# Optimizing a Trainium2 kernel written in Bass

```python
import numpy as np
import jax
import jax.numpy as jnp

def _softmax(x, axis=-1):
    return jax.nn.softmax(x, axis=axis)

def _gelu(x):
    return jax.nn.gelu(x, approximate=True)

def _silu(x):
    return jax.nn.silu(x)

def _sigmoid(x):
    return jax.nn.sigmoid(x)

def _layernorm(x, axis=-1, eps=1e-05):
    m = jnp.mean(x, axis=axis, keepdims=True)
    v = jnp.var(x, axis=axis, keepdims=True)
    return (x - m) / jnp.sqrt(v + eps)

def _scatter_add(tgt, idx, src, axis=0):
    return tgt.at[idx].add(src)

def _segment_sum(src, seg, n):
    return jax.ops.segment_sum(src, seg, n)
kernel_name = 'mk_conv_preact_d2_conv_nhwc768_r4_5d087d'

def setup_inputs(seed: int=0):
    np.random.seed(seed)
    _w = jnp.asarray

    def _rec_inputs():
        import jax
        import jax.numpy as jnp
        _gk = jax.random.key(seed)
        x = -0.0004039 + 1 * jax.random.normal(jax.random.fold_in(_gk, 1), (16, 32, 32, 192), jnp.float32)
        return x
    x = _rec_inputs()

    def _L0_conv_setup():
        import jax, jax.numpy as jnp
        import numpy as np
        NUM_HEADS = 12
        DIM = 192
        HEAD_DIM = DIM // NUM_HEADS
        SCALE = HEAD_DIM ** (-0.5)
        H, W = (32, 32)
        B = 16

        def get_rel_pos(q_size, k_size, rel_pos):
            q_coords = jnp.arange(q_size)[:, None] * max(k_size / q_size, 1.0)
            k_coords = jnp.arange(k_size)[None, :] * max(q_size / k_size, 1.0)
            rel = q_coords - k_coords + (k_size - 1) * max(q_size / k_size, 1.0)
            return rel_pos[rel.astype(jnp.int32)]
        key = jax.random.key(seed)
        ks = jax.random.split(key, 6)
        x = jax.random.normal(ks[0], (B, H, W, DIM), jnp.float32)
        w_qkv = jax.random.normal(ks[1], (3 * DIM, DIM), jnp.float32) * 0.02
        b_qkv = jnp.zeros((3 * DIM,), jnp.float32)
        w_proj = jax.random.normal(ks[2], (DIM, DIM), jnp.float32) * 0.02
        b_proj = jnp.zeros((DIM,), jnp.float32)
        rel_pos_h = jax.random.normal(ks[3], (2 * H - 1, HEAD_DIM), jnp.float32) * 0.02
        rel_pos_w = jax.random.normal(ks[4], (2 * W - 1, HEAD_DIM), jnp.float32) * 0.02
        return {'x': x, 'w_qkv': w_qkv, 'b_qkv': b_qkv, 'w_proj': w_proj, 'b_proj': b_proj, 'rel_pos_h': rel_pos_h, 'rel_pos_w': rel_pos_w}
    _L0_conv_all = _L0_conv_setup()
    _L0_conv_in = {k: v for k, v in _L0_conv_all.items() if k in ('w_qkv', 'b_qkv', 'w_proj', 'b_proj', 'rel_pos_h', 'rel_pos_w')}
    del _L0_conv_all

    def _L1_conv_setup():
        import jax, jax.numpy as jnp
        import numpy as np
        D_MODEL = 192
        D_HEAD = 16
        N_HEADS = D_MODEL // D_HEAD
        KERNEL = 7
        NEG_INF = -1e+30

        def make_neighbourhood_mask(kernel_h, kernel_w, canvas_h, canvas_w):
            h_ramp = jnp.arange(canvas_h)
            w_ramp = jnp.arange(canvas_w)
            h_pos, w_pos = jnp.meshgrid(h_ramp, w_ramp, indexing='ij')
            start_h = jnp.clip(h_pos - kernel_h // 2, 0, canvas_h - kernel_h)[..., None, None]
            end_h = start_h + kernel_h
            start_w = jnp.clip(w_pos - kernel_w // 2, 0, canvas_w - kernel_w)[..., None, None]
            end_w = start_w + kernel_w
            h_range = h_ramp.reshape(1, 1, canvas_h, 1)
            w_range = w_ramp.reshape(1, 1, 1, canvas_w)
            mask = (h_range >= start_h) & (h_range < end_h) & (w_range >= start_w) & (w_range < end_w)
            return mask.reshape(canvas_h * canvas_w, canvas_h * canvas_w)
        key = jax.random.key(seed)
        k1, k2, k3, k4, k5, k6 = jax.random.split(key, 6)
        x = jax.random.normal(k1, (2, 48, 48, D_MODEL), dtype=jnp.float32)
        registers = jax.random.normal(k2, (16, D_MODEL), dtype=jnp.float32)
        scale = 1.0 / np.sqrt(D_MODEL)
        qkv_w = jax.random.normal(k3, (3 * D_MODEL, D_MODEL), dtype=jnp.float32) * scale
        qkv_b = jax.random.normal(k4, (3 * D_MODEL,), dtype=jnp.float32) * 0.01
        out_w = jax.random.normal(k5, (D_MODEL, D_MODEL), dtype=jnp.float32) * scale
        out_b = jax.random.normal(k6, (D_MODEL,), dtype=jnp.float32) * 0.01
        return {'x': x, 'registers': registers, 'qkv_w': qkv_w, 'qkv_b': qkv_b, 'out_w': out_w, 'out_b': out_b}
    _L1_conv_all = _L1_conv_setup()
    _L1_conv_in = {k: v for k, v in _L1_conv_all.items() if k in ('registers', 'qkv_w', 'qkv_b', 'out_w', 'out_b')}
    del _L1_conv_all
    return {'x': x, 'L0_conv_w_qkv': _L0_conv_in['w_qkv'], 'L0_conv_b_qkv': _L0_conv_in['b_qkv'], 'L0_conv_w_proj': _L0_conv_in['w_proj'], 'L0_conv_b_proj': _L0_conv_in['b_proj'], 'L0_conv_rel_pos_h': _L0_conv_in['rel_pos_h'], 'L0_conv_rel_pos_w': _L0_conv_in['rel_pos_w'], 'L1_conv_registers': _L1_conv_in['registers'], 'L1_conv_qkv_w': _L1_conv_in['qkv_w'], 'L1_conv_qkv_b': _L1_conv_in['qkv_b'], 'L1_conv_out_w': _L1_conv_in['out_w'], 'L1_conv_out_b': _L1_conv_in['out_b']}

def reference(x, L0_conv_w_qkv, L0_conv_b_qkv, L0_conv_w_proj, L0_conv_b_proj, L0_conv_rel_pos_h, L0_conv_rel_pos_w, L1_conv_registers, L1_conv_qkv_w, L1_conv_qkv_b, L1_conv_out_w, L1_conv_out_b):
    import jax
    import jax.numpy as jnp

    def _L0_conv_ref(x, w_qkv, b_qkv, w_proj, b_proj, rel_pos_h, rel_pos_w):
        import jax, jax.numpy as jnp
        import numpy as np
        NUM_HEADS = 12
        DIM = 192
        HEAD_DIM = DIM // NUM_HEADS
        SCALE = HEAD_DIM ** (-0.5)
        H, W = (32, 32)
        B = 16

        def get_rel_pos(q_size, k_size, rel_pos):
            q_coords = jnp.arange(q_size)[:, None] * max(k_size / q_size, 1.0)
            k_coords = jnp.arange(k_size)[None, :] * max(q_size / k_size, 1.0)
            rel = q_coords - k_coords + (k_size - 1) * max(q_size / k_size, 1.0)
            return rel_pos[rel.astype(jnp.int32)]
        Bx = x.shape[0]
        S = H * W
        qkv = (x @ w_qkv.T + b_qkv).reshape(Bx, S, 3, NUM_HEADS, HEAD_DIM)
        qkv = jnp.transpose(qkv, (2, 0, 3, 1, 4)).reshape(3, Bx * NUM_HEADS, S, HEAD_DIM)
        q, k, v = (qkv[0], qkv[1], qkv[2])
        Rh = get_rel_pos(H, H, rel_pos_h)
        Rw = get_rel_pos(W, W, rel_pos_w)
        r_q = q.reshape(Bx * NUM_HEADS, H, W, HEAD_DIM)
        rel_h = jnp.einsum('bhwc,hkc->bhwk', r_q, Rh)
        rel_w = jnp.einsum('bhwc,wkc->bhwk', r_q, Rw)
        attn_bias = (rel_h[:, :, :, :, None] + rel_w[:, :, :, None, :]).reshape(Bx * NUM_HEADS, S, S)
        scores = q @ jnp.swapaxes(k, -1, -2) * SCALE + attn_bias
        attn = jax.nn.softmax(scores, axis=-1)
        out = attn @ v
        out = out.reshape(Bx, NUM_HEADS, H, W, HEAD_DIM)
        out = jnp.transpose(out, (0, 2, 3, 1, 4)).reshape(Bx, H, W, DIM)
        return out @ w_proj.T + b_proj

    def _L1_conv_ref(x, registers, qkv_w, qkv_b, out_w, out_b):
        import jax, jax.numpy as jnp
        import numpy as np
        D_MODEL = 192
        D_HEAD = 16
        N_HEADS = D_MODEL // D_HEAD
        KERNEL = 7
        NEG_INF = -1e+30

        def make_neighbourhood_mask(kernel_h, kernel_w, canvas_h, canvas_w):
            h_ramp = jnp.arange(canvas_h)
            w_ramp = jnp.arange(canvas_w)
            h_pos, w_pos = jnp.meshgrid(h_ramp, w_ramp, indexing='ij')
            start_h = jnp.clip(h_pos - kernel_h // 2, 0, canvas_h - kernel_h)[..., None, None]
            end_h = start_h + kernel_h
            start_w = jnp.clip(w_pos - kernel_w // 2, 0, canvas_w - kernel_w)[..., None, None]
            end_w = start_w + kernel_w
            h_range = h_ramp.reshape(1, 1, canvas_h, 1)
            w_range = w_ramp.reshape(1, 1, 1, canvas_w)
            mask = (h_range >= start_h) & (h_range < end_h) & (w_range >= start_w) & (w_range < end_w)
            return mask.reshape(canvas_h * canvas_w, canvas_h * canvas_w)
        n, h, w, _ = x.shape
        nh, e = (N_HEADS, D_HEAD)
        s = h * w
        r = registers.shape[0]
        qkv = x @ qkv_w.T + qkv_b
        qkv = qkv.reshape(n, h, w, 3, nh, e)
        qkv = qkv.transpose(3, 0, 4, 1, 2, 5).reshape(3, n, nh, s, e)
        q, k, v = (qkv[0], qkv[1], qkv[2])
        reg_kv = registers @ qkv_w[D_MODEL:].T + qkv_b[D_MODEL:]
        reg_kv = reg_kv.reshape(r, 2, nh, e).transpose(1, 2, 0, 3)
        reg_k = jnp.broadcast_to(reg_kv[0][None], (n, nh, r, e))
        reg_v = jnp.broadcast_to(reg_kv[1][None], (n, nh, r, e))
        k_cat = jnp.concatenate([k, reg_k], axis=-2)
        v_cat = jnp.concatenate([v, reg_v], axis=-2)
        mask = make_neighbourhood_mask(KERNEL, KERNEL, h, w)
        mask_cat = jnp.concatenate([mask, jnp.ones((s, r), dtype=bool)], axis=-1)
        scale = 1.0 / jnp.sqrt(jnp.asarray(e, dtype=x.dtype))
        scores = jnp.einsum('bnqe,bnke->bnqk', q, k_cat) * scale
        scores = jnp.where(mask_cat[None, None], scores, NEG_INF)
        attn = jax.nn.softmax(scores, axis=-1)
        o = jnp.einsum('bnqk,bnke->bnqe', attn, v_cat)
        o = o.transpose(0, 2, 1, 3).reshape(n, h, w, nh * e)
        return o @ out_w.T + out_b

    def _gn(v, G=32, eps=1e-05):
        B_, H_, W_, C_ = v.shape
        g = v.reshape(B_, H_, W_, G, C_ // G)
        m = jnp.mean(g, axis=(1, 2, 4), keepdims=True)
        s = jnp.var(g, axis=(1, 2, 4), keepdims=True)
        return ((g - m) / jnp.sqrt(s + eps)).reshape(v.shape)

    def _ln_c(v, eps=1e-06):
        m = jnp.mean(v, axis=-1, keepdims=True)
        s = jnp.var(v, axis=-1, keepdims=True)
        return (v - m) / jnp.sqrt(s + eps)

    def _ln_t(v, eps=1e-05):
        m = jnp.mean(v, axis=-1, keepdims=True)
        s = jnp.var(v, axis=-1, keepdims=True)
        return (v - m) / jnp.sqrt(s + eps)

    def _to_tokens(v):
        B_, H_, W_, C_ = v.shape
        return v.reshape(B_, H_ * W_, C_)

    def _from_tokens(t, like):
        return t.reshape(like.shape)
    x = x + _L0_conv_ref(_gn(x), L0_conv_w_qkv, L0_conv_b_qkv, L0_conv_w_proj, L0_conv_b_proj, L0_conv_rel_pos_h, L0_conv_rel_pos_w)
    x = x + _L1_conv_ref(_gn(x), L1_conv_registers, L1_conv_qkv_w, L1_conv_qkv_b, L1_conv_out_w, L1_conv_out_b)
    return x

_drawn_inputs = setup_inputs


def setup_inputs(seed=0):
    import zlib

    import numpy as np

    out = dict(_drawn_inputs(seed))
    spreads = {'L0_conv_b_qkv': (0.0, 0.1), 'L0_conv_b_proj': (0.0, 0.1)}
    factors = {'L0_conv_w_qkv': 8.0,
     'L0_conv_rel_pos_h': 8.0,
     'L0_conv_rel_pos_w': 8.0,
     'L1_conv_qkv_b': 5.846,
     'L1_conv_out_b': 5.48}
    for name, (base, spread) in spreads.items():
        noise = np.random.default_rng([zlib.crc32(name.encode()), seed]).standard_normal(out[name].shape)
        drawn = base * np.exp(spread * noise) if base else spread * noise
        out[name] = jnp.asarray(drawn.astype(out[name].dtype))
    for name, factor in factors.items():
        out[name] = (out[name] * factor).astype(out[name].dtype)
    return out
```

```python
import concourse.bass as bass
from concourse import mybir
from contextlib import ExitStack

B, H, W, C = 16, 32, 32, 192
S = H * W
NH, D = 12, 16
G, GH = 3, 4
TT = S // 128
CH = C // 2
REG = 16
KW = S + 32
WIN = 7
EPS = 1e-5
BIG = 60000.0
ROWS_MAX = (96, 112)
ROWS_LO = 96
NREL = 8
UNITS = (16, 9)
STEPS = (32, 17)
ITEMS = (GH * TT * 2, GH * TT)
RING = 2


def start_row(q):
    return min(max(q - WIN // 2, 0), H - WIN)


def key_rows(qt):
    return start_row(4 * qt), start_row(4 * qt + 3) + WIN


def query_rows(kt):
    seen = [q for q in range(H) if start_row(q) <= 4 * kt + 3 and start_row(q) + WIN > 4 * kt]
    return seen[0], seen[-1] + 1


def max_jobs(layer, image, g, lo=0, hi=None):
    return [(layer, image, g, n) for n in range(lo, ITEMS[layer] + 1 if hi is None else hi)]


def block_stages(i0, i1, n0):
    if i1 is not None:
        yield "prep", 1, i1, None, None
    if i0 is not None:
        yield "main", 0, i0, 0, max_jobs(0, i0, 1)
        yield "main", 0, i0, 1, max_jobs(0, i0, 2)
        yield "main", 0, i0, 2, (max_jobs(1, i1, 0) + max_jobs(1, i1, 1)) if i1 is not None else []
        yield "out", 0, i0, None, None
    elif i1 is not None:
        yield "max", 1, i1, None, max_jobs(1, i1, 0) + max_jobs(1, i1, 1)
    if i1 is not None:
        yield "main", 1, i1, 0, max_jobs(1, i1, 2)
    if n0 is not None:
        yield "prep", 0, n0, None, None
    if i1 is not None:
        half = ITEMS[0] // 2
        yield "main", 1, i1, 1, max_jobs(0, n0, 0, 0, half) if n0 is not None else []
        yield "main", 1, i1, 2, max_jobs(0, n0, 0, half) if n0 is not None else []
        yield "out", 1, i1, None, None
    elif n0 is not None:
        yield "max", 0, n0, None, max_jobs(0, n0, 0)


def before_loop():
    yield "prep", 0, 0, None, None
    yield "max", 0, 0, None, max_jobs(0, 0, 0)
    yield from block_stages(0, None, 1)


def after_loop():
    yield from block_stages(B - 1, B - 2, None)
    yield from block_stages(None, B - 1, None)


def attention_kernel(nc, x, wqkv0, bqkv0, wo0, bo0, relh, relw, regs, wqkv1, bqkv1, wo1, bo1, out):
    F32, F16 = mybir.dt.float32, mybir.dt.float16
    ALU, ACT, AX = mybir.AluOpType, mybir.ActivationFunctionType, mybir.AxisListType
    WQKV, BQKV, WO, BO = (wqkv0, wqkv1), (bqkv0, bqkv1), (wo0, wo1), (bo0, bo1)
    x_t = x.rearrange("b (t r) w c -> b (r w) t c", r=4)
    out_t = out.rearrange("b (t r) w c -> b (r w) t c", r=4)

    ctx = ExitStack()
    with ctx:
        def sb(name, shape, dt=F32):
            return ctx.enter_context(nc.sbuf_tensor(name, shape, dt))

        def sem(name):
            return ctx.enter_context(nc.semaphore(name))

        def sems(name):
            return [sem(f"{name}_l0"), sem(f"{name}_l1")]

        A0, B0, K0 = (sb(n, [128, NH, S], F16) for n in ("A0", "B0", "K0"))
        A1, K1 = sb("A1", [128, NH, S], F16), sb("K1", [128, NH, KW], F16)
        A, K = (A0, A1), (K0, K1)
        V = [sb(f"V{n}", [128, TT, NH, D + 1]) for n in range(2)]
        vreg = sb("vreg", [128, G, 128])
        probs = sb("probs", [128, RING, GH, 512])
        HI = probs[0:CH, 0, :, :].bitcast(F16)
        LO = probs[0:CH, 1, :, :].bitcast(F16)
        HI = HI.rearrange("p m n -> p (m n)").rearrange("p (m n) -> p m n", m=4)
        LO = LO.rearrange("p m n -> p (m n)").rearrange("p (m n) -> p m n", m=4)
        onorm = probs[:, 0, 0:3, :].rearrange("p a n -> p (a n)").rearrange("p (t c) -> p t c", t=TT)
        xin = sb("xin", [128, TT, C])
        xres = sb("xres", [128, TT, C])
        x1 = sb("x1", [128, TT, C])
        xn = sb("xn", [CH + 1, 2, S])
        oraw = sb("oraw", [128, G, S])
        WT = [sb(f"WT{n}", [CH + 1, 2, 3 * C]) for n in range(2)]
        WOT = [sb(f"WOT{n}", [CH + 1, 2, C]) for n in range(2)]
        ident = sb("ident", [128, 128])
        gmat = sb("gmat", [CH, CH])
        regT = sb("regT", [CH + 1, 2, 128])
        RT = sb("RT", [32, 2, 64], F16)
        bn = sb("bn", [CH, 2, 2, 6])
        mv = sb("mv", [CH, 2, 2])
        st = sb("st", [CH, 2, 2])
        gs = sb("gs", [CH, 2, 2])
        nrm = sb("nrm", [CH, 4, 2])
        epsc = sb("epsc", [CH, 2])
        negh = sb("negh", [CH, 4])
        mx = sb("mx", [128, GH * TT, 2])
        mxc = sb("mxc", [128, GH * TT])
        mrow = [sb(f"mrow{n}", [GH * TT, G, 128], F16) for n in range(2)]
        rcp = sb("rcp", [128, 2, 4, NH])
        notlo = sb("notlo", [32, 1])
        wnat = oraw[0:CH, :, :].rearrange("p g n -> p (g n)")[:, 0:6 * C].rearrange("p (m c) -> p m c", m=6)
        wonat = oraw[0:CH, :, :].rearrange("p g n -> p (g n)")[:, 6 * C:8 * C].rearrange("p (m c) -> p m c", m=2)
        rtab = oraw[0:63, :, :].rearrange("p g n -> p (g n)")[:, 1600:1664].rearrange("p (k c) -> p k c", k=2)
        rnat = oraw[:, :, :].rearrange("p g n -> p (g n)")[:, 1700:1892]
        flip = oraw[0:63, :, :].rearrange("p g n -> p (g n)")[:, 1900:1963]
        ktmp = xn[0:32, 0, 0:64].bitcast(F16)
        oneh = probs[0:32, 0, :, :].bitcast(F16).rearrange("p m n -> p (m n)").rearrange("p (m n) -> p m n", m=4)
        mask = probs[0:32, 1, :, :].bitcast(F16).rearrange("p m n -> p (m n)").rearrange("p (m n) -> p m n", m=4)
        ones = x1[0:1, :, :].bitcast(F16).rearrange("p t c -> p (t c)")[:, 0:KW]
        rhi = x1[0:CH, 4, 0:32].bitcast(F16).rearrange("p (c n) -> p c n", c=2)
        rlo = x1[0:CH, 5, 0:32].bitcast(F16).rearrange("p (c n) -> p c n", c=2)

        P = ctx.enter_context(nc.psum_tensor("P", [128, 8, 512], F32))

        def banks(a, n, rows=128):
            return P[0:rows, a:a + n, :].rearrange("p b n -> p (b n)")

        xin_in, xres_in = sem("xin_in"), sem("xres_in")
        xT_done = sems("xT_done")
        dve_chain = sems("dve_chain")
        stat_done = sems("stat_done")
        var_done = sems("var_done")
        gs_done = sems("gs_done")
        pow_done = sems("pow_done")
        nb_done = sems("nb_done")
        xn_act, xn_dve = sems("xn_act"), sems("xn_dve")
        qk_done = sems("qk_done")
        hi_done, lo_done = sems("hi_done"), sems("lo_done")
        v_done = sems("v_done")
        vc_done = sems("vc_done")
        op_in = sems("op_in")
        rel_done, relhi_done, rello_done = sem("rel_done"), sem("relhi_done"), sem("rello_done")
        smax_done = sems("smax_done")
        smax_used = sems("smax_used")
        comb_done = sem("comb_done")
        mrow_in = [[sem(f"mrow_in{g}_l{n}") for g in range(G)] for n in range(2)]
        st_done = sems("st_done")
        p_done = sems("p_done")
        pv_done = sems("pv_done")
        o_done = sems("o_done")
        ot_done = sems("ot_done")
        rcp_done = sems("rcp_done")
        on_done = sems("on_done")
        ob_done = sems("ob_done")
        obc_done = sems("obc_done")
        y_done = sems("y_done")
        res_done = sems("res_done")
        x1_copied = sem("x1_copied")
        out_in = sem("out_in")
        PER_ITEMS = [G * (n + 1) for n in ITEMS]
        PER_STEPS = [G * n for n in STEPS]
        PER_UNITS = [G * n for n in UNITS]
        PER_OP = 36 * 16
        CHAIN = 5
        ROWS_IN = (6 + NH - 1 + 36) * 16
        w_in = sems("w_in")
        tab_in = sem("tab_in")
        scratch_zero = sem("scratch_zero")
        consts_done = sem("consts_done")
        rows_done = sem("rows_done")
        rows_in = sem("rows_in")
        tr_done = sem("tr_done")
        wt_done = sem("wt_done")
        kb_done = sem("kb_done")
        tab_done = sem("tab_done")
        tabhi_done = sem("tabhi_done")
        regT_done = sem("regT_done")
        reg_done = sem("reg_done")
        reghi_done = sem("reghi_done")
        regkv_done = sem("regkv_done")
        dve_set = sem("dve_set")
        pool_chain = sem("pool_chain")

        block = ctx.enter_context(nc.Block())

        SETUP_LOADS = 2 * (6 + 1 + 2 + 1)

        def run_stages(eng, stage):
            for s in before_loop():
                stage(*s)
            with eng.Fori(1, B - 1) as i:
                for s in block_stages(i, i - 1, i + 1):
                    stage(*s)
            for s in after_loop():
                stage(*s)

        def rel_view(r0, b, r, dst, op, other=None):
            src = P[r0:r0 + 32, b:b + 4, 0:NH * 32].rearrange("p b (h w) -> p b h w", h=NH)
            if r0 == 32:
                s = src.rearrange("p b h w -> p h b w")
                pick = lambda t: t[r0:r0 + 32, :, 128 * r:128 * r + 128].rearrange("p h (b w) -> p h b w", b=4)
            else:
                s = src.rearrange("p b h w -> p h w b")
                pick = lambda t: t[r0:r0 + 32, :, :].rearrange("p h (q w) -> p h q w", w=W)[:, :, :, 4 * r:4 * r + 4]
            return op(pick(dst), s) if other is None else op(pick(dst), s, pick(other))

        @block.sync
        def _(sp):
            sp.dma_start(xin[:], x_t[0]).then_inc(xin_in, 16)
            for n in range(2):
                if n:
                    sp.wait_ge(tr_done, 16)
                sp.dma_start(wnat, WQKV[n].rearrange("(m p) c -> p m c", p=CH)).then_inc(w_in[n], 16)
                sp.dma_start(wonat, WO[n].rearrange("(m p) c -> p m c", p=CH)).then_inc(w_in[n], 16)
                sp.dma_start(WT[n][CH:CH + 1, 1, :], BQKV[n].rearrange("(a n) -> a n", a=1)).then_inc(w_in[n], 16)
                sp.dma_start(WOT[n][CH:CH + 1, 1, :], BO[n].rearrange("(a n) -> a n", a=1)).then_inc(w_in[n], 16)
                if n == 0:
                    for k, t in enumerate((relh, relw)):
                        for half in range(2):
                            sp.dma_start(rtab[:, k, half * D:(half + 1) * D], t).then_inc(tab_in, 16)
                    sp.wait_ge(scratch_zero, 1)
                    for j in range(GH):
                        sp.dma_start(rnat[32 * j:32 * j + REG, :], regs).then_inc(tab_in, 16)
            sp.wait_ge(rows_done, 1)
            for r, n in ((32, 0), (64, 1)):
                sp.dma_start(K0[r:r + 32, :, :],
                             oneh[:, n:n + 1, :].broadcast_to((32, NH, S))).then_inc(rows_in, 16)
            for r, n in ((48, 0), (80, 1)):
                sp.dma_start(K1[r:r + 32, :, 0:S],
                             oneh[:, 2 + n:3 + n, :].broadcast_to((32, NH, S))).then_inc(rows_in, 16)
                sp.dma_start(A1[r:r + 32, :, :],
                             mask[:, n:n + 1, :].broadcast_to((32, NH, S))).then_inc(rows_in, 16)
            for h in range(NH):
                sp.dma_start(K1[112:113, h, :], ones).then_inc(rows_in if h < NH - 1 else out_in, 16)
            sp.wait_ge(regkv_done, 1)
            for c in range(2):
                for r, src in ((0, rhi), (16, rlo), (32, rhi)):
                    for hh in range(6):
                        sp.dma_start(K1[r:r + D, 6 * c + hh, S:S + 32],
                                     src[16 * hh:16 * hh + 16, c, :]).then_inc(rows_in, 16)

            def stage(kind, L, im, g, jobs):
                if kind == "prep":
                    base = im * 4
                    rows = (((A[L], 0, HI, 0), (A[L], 16, HI, 0), (B0 if L == 0 else A[L], 0 if L == 0 else 32, LO, 0))
                            + (((B0, 16, LO, 0),) if L == 0 else ()),
                            ((K[L], 0, HI, 2), (K[L], 16, LO, 2)) + (((K[L], 32, HI, 2),) if L else ()))
                    for part, copies in enumerate(rows):
                        sp.wait_ge(lo_done[L], base + 2 * part + 2)
                        for dst, r, src, m in copies:
                            for hh in range(6):
                                sp.dma_start(dst[r:r + D, hh:NH:6, 0:S],
                                             src[16 * hh:16 * hh + 16, m:m + 2, :]).then_inc(op_in[L], 16)
                for layer, image, group, n in jobs or ():
                    if n == ITEMS[layer]:
                        sp.wait_ge(smax_used[layer], image * PER_ITEMS[layer] + (group + 1) * (ITEMS[layer] + 1))
                        r = ROWS_MAX[layer]
                        sp.dma_start(A[layer][r:r + 1, GH * group:GH * group + GH, :],
                                     mrow[layer][:, group, :]).then_inc(mrow_in[layer][group], 16)
                if kind == "main" and L == 0 and g == 1:
                    sp.wait_ge(xT_done[1], im * 2)
                    sp.wait_ge(x1_copied, im)
                    sp.dma_start(xres[:], x_t[im]).then_inc(xres_in, 16)
                if kind == "main" and L == 0 and g == 2 and not (isinstance(im, int) and im == B - 1):
                    sp.wait_ge(xT_done[0], im * 2 + 2)
                    sp.dma_start(xin[:], x_t[im + 1]).then_inc(xin_in, 16)
                if kind == "out" and L == 1:
                    sp.wait_ge(res_done[1], im * 4 + 4)
                    sp.dma_start(out_t[im], x1[:]).then_inc(out_in, 16)

            run_stages(sp, stage)
            sp.wait_ge(out_in, 16 * B + 16)

        @block.gpsimd
        def _(pool):
            step = [0]

            def chained(ins):
                step[0] += 1
                ins.then_inc(pool_chain, 1)
                pool.wait_ge(pool_chain, step[0])

            nc.gpsimd.memset(rnat, 0.0).then_inc(scratch_zero, 1)
            nc.gpsimd.memset(negh[:], -0.5)
            nc.gpsimd.memset(epsc[:], EPS)
            chained(nc.gpsimd.memset(ident[:], 0.0))
            chained(nc.gpsimd.affine_select(out=ident[:], in_=ident[:], compare_op=ALU.not_equal, fill=1.0,
                                            base=0, pattern=[[-1, 128]], channel_multiplier=1))
            chained(nc.gpsimd.memset(flip, 0.0))
            chained(nc.gpsimd.affine_select(out=flip, in_=flip, compare_op=ALU.not_equal, fill=1.0,
                                            base=-62, pattern=[[1, 63]], channel_multiplier=1))
            chained(nc.gpsimd.memset(gmat[:], 1.0 / 6.0))
            gv = gmat[:].rearrange("p (a b) -> p a b", b=6)
            chained(nc.gpsimd.affine_select(out=gv, in_=gv, compare_op=ALU.is_ge, fill=0.0, base=0,
                                            pattern=[[-6, 16], [0, 6]], channel_multiplier=1))
            chained(nc.gpsimd.affine_select(out=gv, in_=gv, compare_op=ALU.is_ge, fill=0.0, base=5,
                                            pattern=[[6, 16], [0, 6]], channel_multiplier=-1))
            chained(nc.gpsimd.memset(notlo[:], -1.0))
            chained(nc.gpsimd.memset(notlo[0:D, :], 0.0))
            chained(nc.gpsimd.memset(regT[CH:CH + 1, :, :], 0.0))
            nc.gpsimd.memset(regT[CH:CH + 1, 1, :].rearrange("p (j r) -> p j r", j=GH)[:, :, 0:REG],
                             1.0).then_inc(consts_done, 1)
            for n, v in ((0, 1.0), (1, 1.0), (2, BIG), (3, BIG)):
                chained(nc.gpsimd.memset(oneh[:, n, :], v))
                o = oneh[:, n, :].rearrange("p (a b) -> p a b", b=W)
                pat = [[-1, H], [0, W]] if n % 2 == 0 else [[0, H], [-1, W]]
                chained(nc.gpsimd.affine_select(out=o, in_=o, compare_op=ALU.is_equal, fill=0.0, base=0,
                                                pattern=pat, channel_multiplier=1))
            R = WIN // 2
            for n in range(2):
                chained(nc.gpsimd.memset(mask[:, n, :], 0.0))
                m = mask[:, n, :].rearrange("p (a b) -> p a b", b=W)

                def select(lo, hi, base, step_q, cm):
                    sub = m[:, lo:hi, :] if n == 0 else m[:, :, lo:hi]
                    pat = [[step_q, hi - lo], [0, W]] if n == 0 else [[0, H], [step_q, hi - lo]]
                    chained(nc.gpsimd.affine_select(out=sub, in_=sub, compare_op=ALU.is_ge, fill=-BIG,
                                                    base=base, pattern=pat, channel_multiplier=cm))

                select(0, R + 1, WIN - 1, 0, -1)
                select(H - R - 1, H, WIN - H, 0, 1)
                select(R + 1, H - R - 1, R - (R + 1), -1, 1)
                select(R + 1, H - R - 1, R + (R + 1), 1, -1)
            nc.gpsimd.memset(ones, 1.0).then_inc(rows_done, 1)

            def take_wait():
                nc.gpsimd.tensor_tensor(negh[:, 1:2], negh[:, 0:1], negh[:, 2:3], ALU.mult)

            def stage(kind, L, im, g, jobs):
                if kind != "prep":
                    return
                if L == 1:
                    pool.wait_ge(res_done[0], im * 4 + 4)
                    pool.wait_ge(out_in, im * 16 + 16)
                    take_wait()
                    nc.gpsimd.tensor_copy(x1[:], xres[:]).then_inc(x1_copied, 1)
                pool.wait_ge(var_done[L], im + 1)
                nc.gpsimd.tensor_tensor(nrm[:, 1, :], nrm[:, 1, :], epsc[:], ALU.add).then_inc(pow_done[L], 1)
                pool.wait_ge(pow_done[L], im * 2 + 1)
                nc.gpsimd.tensor_tensor(nrm[:, 2, :], nrm[:, 1, :], negh[:, 2:4], ALU.pow).then_inc(pow_done[L], 1)

            run_stages(pool, stage)

        @block.scalar
        def _(act):
            def copy(out_, in_, scale=1.0):
                return nc.scalar.activation(out_, in_, ACT.Copy, scale=scale)

            for n in range(2):
                act.wait_ge(w_in[n], 16 * 4)
                copy(WT[n][CH:CH + 1, 1, C:2 * C], WT[n][CH:CH + 1, 1, C:2 * C], D ** -0.5).then_inc(kb_done, 1)
                for t in range(16):
                    m, c = t // 2, t % 2
                    act.wait_ge(tr_done, 16 * n + t + 1)
                    src = P[0:CH, t % 4, 0:CH]
                    if m < 6:
                        copy(WT[n][0:CH, c, m * CH:(m + 1) * CH], src,
                             D ** -0.5 if m in (2, 3) else 1.0).then_inc(wt_done, 1)
                    else:
                        copy(WOT[n][0:CH, c, (m - 6) * CH:(m - 5) * CH], src).then_inc(wt_done, 1)
            act.wait_ge(rows_in, ROWS_IN)
            prepared = []

            def probs_free():
                while prepared:
                    L, im = prepared.pop()
                    act.wait_ge(op_in[L], (im + 1) * PER_OP)

            def stage(kind, L, im, g, jobs):
                if kind == "prep":
                    act.wait_ge(nb_done[L], im + 1)
                    nc.scalar.activation(xn[0:CH, 0, :], banks(0, 2, CH), ACT.Identity,
                                         bias=nrm[:, 3, 0:1], scale=nrm[:, 2, 0:1]).then_inc(xn_act[L], 1)
                    for m, b in enumerate((6, 4, 0, 2)):
                        act.wait_ge(qk_done[L], im * 4 + m + 1)
                        copy(HI[:, m, :], banks(b, 2, CH)).then_inc(hi_done[L], 1)
                    for n, b in enumerate((6, 7, 4, 5)):
                        act.wait_ge(v_done[L], im * 4 + n + 1)
                        copy(V[L][:, 2 * n:2 * n + 2, :, 0:D],
                             P[:, b, 0:2 * C].rearrange("p (t h d) -> p t h d", t=2, h=NH)).then_inc(vc_done[L], 1)
                    for r in range(NREL if L == 0 else 0):
                        act.wait_ge(rel_done, im * NREL + r + 1)
                        b = 4 * (r % 2)
                        rel_view(32, b, r, A0, lambda d, s: copy(d, s))
                        rel_view(64, b, r, A0, lambda d, s: copy(d, s)).then_inc(relhi_done, 1)
                    prepared.append((L, im))
                if kind in ("main", "max"):
                    probs_free()
                if kind == "main":
                    base, ubase = im * PER_STEPS[L] + g * STEPS[L], im * PER_UNITS[L] + g * UNITS[L]
                    step = 0
                    for u in range(UNITS[L]):
                        if u >= RING:
                            act.wait_ge(pv_done[L], ubase + u - RING + 1)
                        for part in range(1 if L and u == 0 else 2):
                            act.wait_ge(st_done[L], base + step + 1)
                            b = 2 * (step % 2)
                            n = 512 if L == 0 or u == 0 else W * (query_rows(u - 1)[1] - query_rows(u - 1)[0])
                            nc.scalar.activation(probs[:, u % RING, 2 * part:2 * part + 2, 0:n], P[:, b:b + 2, 0:n],
                                                 ACT.Exp).then_inc(p_done[L], 1)
                            step += 1
                        if L == 0 and u == TT + 1:
                            copy_out(L, im, g, ubase, 0)
                    for half in ((1,) if L == 0 else (0, 1)):
                        copy_out(L, im, g, ubase, half)
                if kind == "out":
                    for half in range(2):
                        act.wait_ge(ob_done[L], im * 2 + half + 1)
                        copy(xn[0:CH, :, half * 512:(half + 1) * 512],
                             P[0:CH, 2 * half:2 * half + 2, :]).then_inc(obc_done[L], 1)

            def copy_out(L, im, g, ubase, half):
                act.wait_ge(pv_done[L], ubase + ((half + 1) * TT if L == 0 else UNITS[1]))
                copy(oraw[:, g, half * 512:(half + 1) * 512], P[:, 6 + half, :]).then_inc(o_done[L], 1)

            run_stages(act, stage)

        @block.vector
        def _(dve):
            V_ = nc.vector
            V_.memset(xn[CH:CH + 1, :, :], 1.0)
            V_.memset(P[:, 6:8, :], 0.0)
            V_.memset(K0[96:97, :, :], 1.0)
            V_.memset(K1[0:64, :, S:KW], 0.0)
            V_.memset(K1[64:112, :, S:KW], 0.0)
            for n in range(2):
                V_.memset(V[n][:, :, :, D:D + 1], 1.0)
            V_.memset(vreg[:], 0.0).then_inc(dve_set, 1)
            dve.wait_ge(dve_set, 1)
            for j in range(GH):
                V_.memset(vreg[32 * j:32 * j + REG, :, 32 * j + D:32 * j + D + 1], 1.0).then_inc(dve_set, 1)
            dve.wait_ge(tab_done, 1)
            for k in range(2):
                V_.tensor_copy(ktmp[:, 64 * k:64 * k + 63], P[0:32, 4 + k, 0:63]).then_inc(tabhi_done, 1)
            dve.wait_ge(tabhi_done, 2)
            for k in range(2):
                V_.scalar_tensor_tensor(RT[:, k, 0:63], ktmp[:, 64 * k:64 * k + 63], notlo[:, 0:1],
                                        P[0:32, 4 + k, 0:63], ALU.mult, ALU.add)
            V_.tensor_copy(regT[0:CH, :, :], P[0:CH, 4:6, 128:256]).then_inc(regT_done, 1)
            dve.wait_ge(reg_done, 1)
            for c in range(2):
                V_.tensor_copy(rhi[:, c, :], P[0:CH, c, 0:32]).then_inc(reghi_done, 1)
            dve.wait_ge(reghi_done, 2)
            for c in range(2):
                V_.tensor_tensor(rlo[:, c, :], P[0:CH, c, 0:32], rhi[:, c, :], ALU.subtract)
            for j in range(GH):
                r = slice(32 * j, 32 * j + 32)
                last = V_.tensor_copy(vreg[r, :, 32 * j:32 * j + D],
                                      P[r, 2, 0:C].rearrange("p (g c) -> p g c", g=G)[:, :, D * j:D * j + D])
            last.then_inc(regkv_done, 1)

            def stage(kind, L, im, g, jobs):
                step = [0]

                def chained(ins):
                    step[0] += 1
                    ins.then_inc(dve_chain[L], 1)
                    dve.wait_ge(dve_chain[L], im * CHAIN + step[0])

                if kind == "prep":
                    for c in range(2):
                        dve.wait_ge(xT_done[L], im * 2 + c + 1)
                        for half in range(2):
                            ins = V_.bn_stats(bn[:, c, half, :], P[0:CH, 2 * c + half, :])
                    chained(ins)
                    V_.memset(nrm[:, 0, 0:1], 0.0)
                    for c in range(2):
                        ins = V_.bn_aggr(mv[:, c, :], bn[:, c, :, :].rearrange("p a b -> p (a b)"))
                    chained(ins)
                    chained(V_.tensor_tensor(nrm[:, 0, :], mv[:, :, 0], mv[:, :, 0], ALU.mult))
                    V_.tensor_tensor(st[:, :, 1], nrm[:, 0, :], mv[:, :, 1], ALU.add)
                    V_.tensor_copy(st[:, :, 0], mv[:, :, 0]).then_inc(stat_done[L], 1)
                    dve.wait_ge(gs_done[L], im + 1)
                    chained(V_.tensor_copy(gs[:].rearrange("p a b -> p (a b)"), P[0:CH, 4, 0:4]))
                    chained(V_.tensor_tensor(nrm[:, 0, :], gs[:, :, 0], gs[:, :, 0], ALU.mult))
                    V_.tensor_tensor(nrm[:, 1, :], gs[:, :, 1], nrm[:, 0, :], ALU.subtract).then_inc(var_done[L], 1)
                    dve.wait_ge(pow_done[L], im * 2 + 2)
                    V_.scalar_tensor_tensor(nrm[:, 3, :], gs[:, :, 0], -1.0, nrm[:, 2, :],
                                            ALU.mult, ALU.mult).then_inc(nb_done[L], 1)
                    dve.wait_ge(nb_done[L], im + 1)
                    V_.tensor_scalar(xn[0:CH, 1, :], banks(2, 2, CH), nrm[:, 2, 1:2], nrm[:, 3, 1:2],
                                     ALU.mult, ALU.add).then_inc(xn_dve[L], 1)
                    assert step[0] == 5
                    for m, b in enumerate((6, 4, 0, 2)):
                        dve.wait_ge(hi_done[L], im * 4 + m + 1)
                        V_.tensor_tensor(LO[:, m, :], banks(b, 2, CH), HI[:, m, :],
                                         ALU.subtract).then_inc(lo_done[L], 1)
                    for r in range(NREL if L == 0 else 0):
                        dve.wait_ge(relhi_done, im * NREL + r + 1)
                        low = lambda d, s, a: V_.tensor_tensor(d, s, a, ALU.subtract)
                        rel_view(32, 4 * (r % 2), r, B0, low, A0)
                        rel_view(64, 4 * (r % 2), r, B0, low, A0).then_inc(rello_done, 1)
                for at, (layer, image, group, n) in enumerate(jobs or ()):
                    base = image * PER_ITEMS[layer] + group * (ITEMS[layer] + 1)
                    dve.wait_ge(smax_done[layer], base + n + 1)
                    bank = P[:, 4 + at % 2, :]
                    if n == ITEMS[layer]:
                        V_.tensor_scalar(mrow[layer][:, group, :], bank[0:GH * TT, 0:128], -1.0, None,
                                         ALU.mult).then_inc(smax_used[layer], 1)
                    elif layer == 0:
                        V_.reduce_max(mx[:, n // 2, n % 2:n % 2 + 1], bank, AX.X).then_inc(smax_used[0], 1)
                        if n == ITEMS[0] - 1:
                            dve.wait_ge(smax_used[0], base + ITEMS[0])
                            V_.tensor_reduce(mxc[:], mx[:], AX.X, ALU.max).then_inc(comb_done, 1)
                    else:
                        lo, hi = key_rows(n % TT)
                        V_.reduce_max(mxc[:, n:n + 1], bank[:, 0:W * (hi - lo) + REG],
                                      AX.X).then_inc(smax_used[1], 1)
                if kind == "out":
                    for q in range(2):
                        dve.wait_ge(ot_done[L], im * TT + 4 * q + 4)
                        src = P[:, 4 * q:4 * q + 4, 0:NH * 32].rearrange("p t (h r) -> p t h r", r=32)
                        V_.reciprocal(rcp[:, q, :, :], src[:, :, :, D]).then_inc(rcp_done[L], 1)
                        dve.wait_ge(rcp_done[L], im * 2 + q + 1)
                        V_.tensor_tensor(onorm[:, 4 * q:4 * q + 4, :].rearrange("p t (h d) -> p t h d", h=NH),
                                         src[:, :, :, 0:D],
                                         rcp[:, q, :, :].unsqueeze(3).broadcast_to((128, 4, NH, D)),
                                         ALU.mult).then_inc(on_done[L], 1)
                    acc = xres if L == 0 else x1
                    if L == 0:
                        dve.wait_ge(xres_in, im * 16 + 16)
                    else:
                        dve.wait_ge(x1_copied, im + 1)
                    for b in range(4):
                        dve.wait_ge(y_done[L], im * 4 + b + 1)
                        V_.tensor_tensor(acc[:, 2 * b:2 * b + 2, :], P[:, 4 + b, 0:2 * C].rearrange("p (t c) -> p t c", t=2),
                                         acc[:, 2 * b:2 * b + 2, :], ALU.add).then_inc(res_done[L], 1)

            run_stages(dve, stage)

        @block.tensor
        def _(pe):
            mm = nc.tensor.matmul

            def chunks(out_, lhs, rhs):
                mm(out_, lhs(CH, 0), rhs(CH, 0), start=True, stop=False)
                return mm(out_, lhs(CH + 1, 1), rhs(CH + 1, 1), start=False, stop=True)

            pe.wait_ge(consts_done, 1)
            for n in range(2):
                pe.wait_ge(w_in[n], 16 * 4)
                for t in range(16):
                    m, c = t // 2, t % 2
                    if 16 * n + t >= 4:
                        pe.wait_ge(wt_done, 16 * n + t - 3)
                    src = wnat[:, m, :] if m < 6 else wonat[:, m - 6, :]
                    nc.tensor.transpose(P[0:CH, t % 4, 0:CH], src[:, c * CH:(c + 1) * CH],
                                        ident[0:CH, 0:CH]).then_inc(tr_done, 1)
                if n == 0:
                    pe.wait_ge(tab_in, 16 * 8)
                    for k in range(2):
                        mm(P[0:32, 4 + k, 0:63], rtab[:, k, :], flip, start=True, stop=True)
                        last = nc.tensor.transpose(P[0:CH, 4 + k, 128:256], rnat[:, k * CH:(k + 1) * CH], ident[:])
                    last.then_inc(tab_done, 1)
            pe.wait_ge(wt_done, 32)
            pe.wait_ge(kb_done, 2)
            pe.wait_ge(regT_done, 1)
            for c in range(2):
                chunks(P[0:CH, c, 0:32], lambda k, s: WT[1][0:k, s, C + c * CH:C + (c + 1) * CH],
                       lambda k, s: regT[0:k, s, 0:32])
            chunks(P[:, 2, 0:C], lambda k, s: regT[0:k, s, :],
                   lambda k, s: WT[1][0:k, s, 2 * C:3 * C]).then_inc(reg_done, 1)
            pe.wait_ge(regkv_done, 1)
            pe.wait_ge(rows_in, ROWS_IN)
            pe.wait_ge(out_in, 16)

            def project(L, im):
                src = xin if L == 0 else xres
                if L == 0:
                    pe.wait_ge(xin_in, im * 16 + 16)
                else:
                    pe.wait_ge(res_done[0], im * 4 + 4)
                for c in range(2):
                    for t in range(TT):
                        last = nc.tensor.transpose(P[0:CH, 2 * c + t // 4, 128 * (t % 4):128 * (t % 4) + 128],
                                                   src[:, t, c * CH:(c + 1) * CH], ident[:])
                    last.then_inc(xT_done[L], 1)
                pe.wait_ge(stat_done[L], im + 1)
                mm(P[0:CH, 4, 0:4], gmat[:], st[:].rearrange("p a b -> p (a b)"),
                   start=True, stop=True).then_inc(gs_done[L], 1)
                pe.wait_ge(xn_act[L], im + 1)
                pe.wait_ge(xn_dve[L], im + 1)
                for m, b in enumerate((6, 4, 0, 2)):
                    for half in range(2):
                        last = chunks(P[0:CH, b + half, :],
                                      lambda k, s: WT[L][0:k, s, m * CH:(m + 1) * CH],
                                      lambda k, s: xn[0:k, s, half * 512:(half + 1) * 512])
                    last.then_inc(qk_done[L], 1)
                for n, b in enumerate((6, 7, 4, 5)):
                    pe.wait_ge(lo_done[L], im * 4 + 1 + n // 2)
                    for t in (2 * n, 2 * n + 1):
                        last = chunks(P[:, b, (t % 2) * C:(t % 2 + 1) * C],
                                      lambda k, s: xn[0:k, s, 128 * t:128 * t + 128],
                                      lambda k, s: WT[L][0:k, s, 2 * C:3 * C])
                    last.then_inc(v_done[L], 1)
                if L == 0:
                    pe.wait_ge(op_in[0], (im + 1) * PER_OP)
                    for r in range(NREL):
                        if r == 0:
                            pe.wait_ge(lo_done[0], im * 4 + 4)
                        elif r == 1:
                            pe.wait_ge(vc_done[0], im * 4 + 4)
                        else:
                            pe.wait_ge(rello_done, im * NREL + r - 1)
                        mm(P[0:32, 4 * (r % 2), 0:1], ident[:, 0:32], ident[:, 0:1], start=True, stop=True)
                        for bb in range(4):
                            row = 4 * r + bb
                            for q, first in ((A0, True), (B0, False)):
                                for k, rhs in ((0, q[0:32, :, row * W:(row + 1) * W]), (1, q[0:32, :, row:S:W])):
                                    last = mm(P[32 + 32 * k:64 + 32 * k, 4 * (r % 2) + bb, 0:NH * 32],
                                              RT[:, k, H - 1 - row:2 * H - 1 - row], rhs,
                                              start=first, stop=not first)
                        last.then_inc(rel_done, 1)
                    pe.wait_ge(rello_done, (im + 1) * NREL)
                pe.wait_ge(lo_done[L], im * 4 + 4)
                pe.wait_ge(vc_done[L], im * 4 + 4)

            def job_base(layer, image, group):
                return image * PER_ITEMS[layer] + group * (ITEMS[layer] + 1)

            def max_item(jobs, at):
                layer, image, group, n = jobs[at]
                base = job_base(layer, image, group)
                if at >= 2:
                    pl, pi, pg, pn = jobs[at - 2]
                    pe.wait_ge(smax_used[pl], job_base(pl, pi, pg) + pn + 1)
                if n == 0 and group == 0:
                    pe.wait_ge(op_in[layer], (image + 1) * PER_OP)
                bank = P[:, 4 + at % 2, :]
                if n == ITEMS[layer]:
                    if layer == 0:
                        pe.wait_ge(comb_done, image * G + group + 1)
                    else:
                        pe.wait_ge(smax_used[1], base + ITEMS[1])
                    last = nc.tensor.transpose(bank[0:GH * TT, 0:128], mxc[:], ident[:])
                elif layer == 0:
                    h, qt, half = GH * group + n // (2 * TT), n // 2 % TT, n % 2
                    last = mm(bank, A0[0:ROWS_MAX[0], h, 128 * qt:128 * qt + 128],
                              K0[0:ROWS_MAX[0], h, half * 512:(half + 1) * 512], start=True, stop=True)
                else:
                    h, qt = GH * group + n // TT, n % TT
                    lo, hi = key_rows(qt)
                    cols = W * (hi - lo)
                    lhs = A1[0:ROWS_MAX[1], h, 128 * qt:128 * qt + 128]
                    mm(bank[:, 0:cols], lhs, K1[0:ROWS_MAX[1], h, W * lo:W * hi], start=True, stop=True)
                    last = mm(bank[:, cols:cols + REG], lhs, K1[0:ROWS_MAX[1], h, S:S + REG], start=True, stop=True)
                last.then_inc(smax_done[layer], 1)

            def jobs_read(jobs):
                if jobs:
                    layer, image, group, n = jobs[-1]
                    pe.wait_ge(smax_used[layer], job_base(layer, image, group) + n + 1)

            def attend(L, im, g, jobs):
                base, ubase = im * PER_STEPS[L] + g * STEPS[L], im * PER_UNITS[L] + g * UNITS[L]
                pe.wait_ge(mrow_in[L][g], im * 16 + 16)
                R = ROWS_MAX[L] + 1
                step, sent = 0, 0
                ends = []

                def use(u):
                    pe.wait_ge(p_done[L], base + ends[u])
                    slot = u % RING
                    if L == 0:
                        half, kt = u // TT, u % TT
                        for j in range(GH):
                            last = mm(P[32 * j:32 * j + D + 1, 6 + half, :], V[0][:, kt, GH * g + j, :],
                                      probs[:, slot, j, :], start=(kt == 0), stop=(kt == TT - 1))
                    elif u == 0:
                        for half in range(2):
                            last = mm(P[:, 6 + half, :], vreg[:, g, :], probs[:, slot, half, :],
                                      start=True, stop=False, skip_group_check=True)
                    else:
                        kt = u - 1
                        lo, hi = (W * r for r in query_rows(kt))
                        for half in range(2):
                            a, b = max(lo, 512 * half), min(hi, 512 * half + 512)
                            for j in range(GH if a < b else 0):
                                last = mm(P[32 * j:32 * j + D + 1, 6 + half, a - 512 * half:b - 512 * half],
                                          V[1][:, kt, GH * g + j, :], probs[:, slot, j, a - lo:b - lo],
                                          start=False, stop=(u == UNITS[1] - 1), skip_group_check=True)
                    last.then_inc(pv_done[L], 1)

                for u in range(UNITS[L]):
                    for part in range(1 if L and u == 0 else 2):
                        if step >= 2:
                            pe.wait_ge(p_done[L], base + step - 1)
                        b = 2 * (step % 2)
                        if L == 1 and u == 0:
                            for half in range(2):
                                for j in range(GH):
                                    h = GH * g + j
                                    last = mm(P[32 * j:32 * j + 32, b + half, :], K1[0:R, h, S:KW],
                                              A1[0:R, h, 512 * half:512 * half + 512], start=True, stop=True)
                        for jj in range(0 if L == 1 and u == 0 else 2):
                            h = GH * g + 2 * part + jj
                            if L == 0:
                                half, kt = u // TT, u % TT
                                q = slice(512 * half, 512 * half + 512)
                                k = slice(128 * kt, 128 * kt + 128)
                                mm(P[:, b + jj, :], K0[0:R, h, k], A0[0:R, h, q], start=True, stop=False)
                                last = mm(P[:, b + jj, :], K0[0:ROWS_LO, h, k], B0[0:ROWS_LO, h, q],
                                          start=False, stop=True)
                            else:
                                lo, hi = (W * r for r in query_rows(u - 1))
                                last = mm(P[:, b + jj, 0:hi - lo], K1[0:R, h, 128 * (u - 1):128 * u],
                                          A1[0:R, h, lo:hi], start=True, stop=True)
                        last.then_inc(st_done[L], 1)
                        step += 1
                        while sent < len(jobs) and sent * (STEPS[L] - 2) < len(jobs) * step:
                            max_item(jobs, sent)
                            sent += 1
                    ends.append(step)
                    if u:
                        use(u - 1)
                use(UNITS[L] - 1)
                while sent < len(jobs):
                    max_item(jobs, sent)
                    sent += 1
                jobs_read(jobs)
                pe.wait_ge(o_done[L], im * 6 + 2 * g + 2)

            def deliver(L, im):
                for t in range(TT):
                    for g in range(G):
                        last = nc.tensor.transpose(P[:, t, 128 * g:128 * g + 128],
                                                   oraw[:, g, 128 * t:128 * t + 128], ident[:])
                    last.then_inc(ot_done[L], 1)
                for q in range(2):
                    pe.wait_ge(on_done[L], im * 2 + q + 1)
                    for t in range(4 * q, 4 * q + 4):
                        for c in range(2):
                            last = nc.tensor.transpose(P[0:CH, 2 * q + c, 128 * (t % 4):128 * (t % 4) + 128],
                                                       onorm[:, t, c * CH:(c + 1) * CH], ident[:])
                    last.then_inc(ob_done[L], 1)
                for b in range(4):
                    pe.wait_ge(obc_done[L], im * 2 + b // 2 + 1)
                    for t in (2 * b, 2 * b + 1):
                        last = chunks(P[:, 4 + b, (t % 2) * C:(t % 2 + 1) * C],
                                      lambda k, s: xn[0:k, s, 128 * t:128 * t + 128],
                                      lambda k, s: WOT[L][0:k, s, :])
                    last.then_inc(y_done[L], 1)
                pe.wait_ge(res_done[L], im * 4 + 4)

            def stage(kind, L, im, g, jobs):
                if kind == "prep":
                    project(L, im)
                if kind == "max":
                    for at in range(len(jobs)):
                        max_item(jobs, at)
                    jobs_read(jobs)
                if kind == "main":
                    attend(L, im, g, jobs)
                if kind == "out":
                    deliver(L, im)

            run_stages(pe, stage)


_INS = ["x", "L0_conv_w_qkv", "L0_conv_b_qkv", "L0_conv_w_proj", "L0_conv_b_proj", "L0_conv_rel_pos_h",
        "L0_conv_rel_pos_w", "L1_conv_registers", "L1_conv_qkv_w", "L1_conv_qkv_b", "L1_conv_out_w",
        "L1_conv_out_b"]


def kernel(**inputs):
    import numpy as _np
    import concourse.bacc as _bacc
    from concourse import mybir as _mybir
    from concourse.bass_utils import run_bass_kernel_spmd as _run

    nc = _bacc.Bacc("TRN2", target_bir_lowering=False, num_devices=1)
    arrays, args = {}, []
    for name in _INS:
        a = _np.ascontiguousarray(inputs[name])
        arrays[f"in_{name}_dram"] = a
        args.append(nc.dram_tensor(f"in_{name}_dram", a.shape, _mybir.dt.from_np(a.dtype), kind="ExternalInput").ap())
    out = nc.dram_tensor("out_0_dram", (B, H, W, C), _mybir.dt.float32, kind="ExternalOutput").ap()
    attention_kernel(nc, *args, out)
    r = _run(nc, [arrays], core_ids=[0])
    return r.results[0]["out_0_dram"]
```

```python
import concourse.bass as bass
from concourse import mybir
from contextlib import ExitStack

B, H, W, C = 16, 32, 32, 192
S = H * W
NH, D = 12, 16
G, GH = 3, 4
TT = S // 128
CH = C // 2
REG = 16
KW = S + 32
WIN = 7
EPS = 1e-5
BIG = 60000.0
ROWS_MAX = (96, 112)
ROWS_LO = 96
GC = GH * D
RELS = H // 4
UNITS = (16, 9)
STEPS = (32, 17)
ITEMS = (GH * TT * 2, GH * TT)
SKIP = (0, 0)
RING = 2


def start_row(q):
    return min(max(q - WIN // 2, 0), H - WIN)


def key_rows(qt):
    return start_row(4 * qt), start_row(4 * qt + 3) + WIN


def query_rows(kt):
    seen = [q for q in range(H) if start_row(q) <= 4 * kt + 3 and start_row(q) + WIN > 4 * kt]
    return seen[0], seen[-1] + 1


def max_jobs(layer, image, g):
    return [("max", layer, image, g, n) for n in range(ITEMS[layer] + 1)]


def rel_jobs(image, g):
    return [("rel", 0, image, g, n) for n in range(RELS)]


def work(jobs):
    return sum(12 if j[0] == "rel" else (6, 4)[j[1]] for j in jobs)


def paced(jobs, steps, skip):
    full, lo, hi = jobs
    room = 2 * steps - 3 - skip
    after = [[] for _ in range(2 * steps)]
    for k in range(lo, hi):
        after[skip + work(full[lo:k]) * room // work(full[lo:hi])].append(k)
    return after


def mains(layer, image, *parts):
    full, at = sum(parts, []), 0
    for g, part in enumerate(parts):
        yield "main", layer, image, g, (full, at, at + len(part))
        at += len(part)


def thirds(jobs):
    cuts = [[k for k in range(len(jobs)) if work(jobs[:k]) * G // work(jobs) == m] for m in range(G)]
    return [[jobs[k] for k in c] for c in cuts]


def block_stages(i0, i1, n0):
    none = ([], 0, 0)
    coming = rel_jobs(n0, 0) + max_jobs(0, n0, 0) if n0 is not None else []
    first = sum((max_jobs(1, i1, g) for g in range(G)), []) if i1 is not None else []
    if i1 is not None:
        yield "prep", 1, i1, None, none
    if i0 is not None:
        yield from mains(0, i0, rel_jobs(i0, 1) + max_jobs(0, i0, 1), rel_jobs(i0, 2) + max_jobs(0, i0, 2), first)
        yield "out", 0, i0, None, none
    else:
        yield "jobs", 1, i1, None, (first, 0, len(first))
    if n0 is not None:
        yield "prep", 0, n0, None, none
    if i1 is not None:
        yield from mains(1, i1, *thirds(coming))
        yield "out", 1, i1, None, none
    else:
        yield "jobs", 0, n0, None, (coming, 0, len(coming))


def before_loop():
    coming = rel_jobs(0, 0) + max_jobs(0, 0, 0)
    yield "prep", 0, 0, None, ([], 0, 0)
    yield "jobs", 0, 0, None, (coming, 0, len(coming))
    yield from block_stages(0, None, 1)


def after_loop():
    yield from block_stages(B - 1, B - 2, None)
    yield from block_stages(None, B - 1, None)


def attention_kernel(nc, x, wqkv0, bqkv0, wo0, bo0, relh, relw, regs, wqkv1, bqkv1, wo1, bo1, out):
    F32, F16 = mybir.dt.float32, mybir.dt.float16
    ALU, ACT, AX = mybir.AluOpType, mybir.ActivationFunctionType, mybir.AxisListType
    WQKV, BQKV, WO, BO = (wqkv0, wqkv1), (bqkv0, bqkv1), (wo0, wo1), (bo0, bo1)
    x_t = x.rearrange("b (t r) w c -> b (r w) t c", r=4)
    out_t = out.rearrange("b (t r) w c -> b (r w) t c", r=4)

    ctx = ExitStack()
    with ctx:
        def sb(name, shape, dt=F32):
            return ctx.enter_context(nc.sbuf_tensor(name, shape, dt))

        def sem(name):
            return ctx.enter_context(nc.semaphore(name))

        def sems(name):
            return [sem(f"{name}_l0"), sem(f"{name}_l1")]

        A0, B0, K0 = (sb(n, [128, NH, S], F16) for n in ("A0", "B0", "K0"))
        A1, K1 = sb("A1", [128, NH, S], F16), sb("K1", [128, NH, KW], F16)
        A, K = (A0, A1), (K0, K1)
        V = [sb(f"V{n}", [128, TT, NH, D + 1]) for n in range(2)]
        vreg = sb("vreg", [128, G, 128])
        probs = sb("probs", [128, RING, GH, 512])
        onorm = probs[:, 0, 0:3, :].rearrange("p a n -> p (a n)").rearrange("p (t c) -> p t c", t=TT)
        xin = sb("xin", [128, TT, C])
        xres = sb("xres", [128, TT, C])
        x1 = sb("x1", [128, TT, C])
        xn = sb("xn", [CH + 1, 2, S])
        oraw = sb("oraw", [128, G, S])
        flat = oraw[:].rearrange("p g n -> p (g n)")
        HI = flat[:, 0:G * S // 2].bitcast(F16).rearrange("p (g n) -> p g n", g=G)
        LO = flat[:, G * S // 2:G * S].bitcast(F16).rearrange("p (g n) -> p g n", g=G)
        WT = [sb(f"WT{n}", [CH + 1, 2, 3 * C]) for n in range(2)]
        WOT = [sb(f"WOT{n}", [CH + 1, 2, C]) for n in range(2)]
        ident = sb("ident", [128, 128])
        gmat = sb("gmat", [CH, CH])
        regT = sb("regT", [CH + 1, 2, 128])
        RT = sb("RT", [32, 2, 64], F16)
        bn = sb("bn", [CH, 2, 2, 6])
        mv = sb("mv", [CH, 2, 2])
        st = sb("st", [CH, 2, 2])
        gs = sb("gs", [CH, 2, 2])
        nrm = sb("nrm", [CH, 4, 2])
        epsc = sb("epsc", [CH, 2])
        negh = sb("negh", [CH, 4])
        mx = sb("mx", [128, GH * TT, 2])
        mxc = sb("mxc", [128, GH * TT])
        mrow = [sb(f"mrow{n}", [GH * TT, G, 128], F16) for n in range(2)]
        rcp = sb("rcp", [128, 2, 4, NH])
        notlo = sb("notlo", [32, 1])
        wnat = flat[0:GC, 0:9 * C].rearrange("p (m c) -> p m c", m=9)
        wonat = flat[0:GC, 9 * C:12 * C].rearrange("p (m c) -> p m c", m=3)
        rtab = flat[0:63, 12 * C:12 * C + 64].rearrange("p (k c) -> p k c", k=2)
        rnat = flat[:, 13 * C:14 * C]
        flip = flat[0:63, 14 * C:14 * C + 63]
        ktmp = xn[0:32, 0, 0:64].bitcast(F16)
        oneh = probs[0:32, 0, :, :].bitcast(F16).rearrange("p m n -> p (m n)").rearrange("p (m n) -> p m n", m=4)
        mask = probs[0:32, 1, :, :].bitcast(F16).rearrange("p m n -> p (m n)").rearrange("p (m n) -> p m n", m=4)
        ones = x1[0:1, :, :].bitcast(F16).rearrange("p t c -> p (t c)")[:, 0:KW]
        rhi = x1[0:GC, 4, 0:48].bitcast(F16).rearrange("p (g n) -> p g n", g=G)
        rlo = x1[0:GC, 5, 0:48].bitcast(F16).rearrange("p (g n) -> p g n", g=G)

        P = ctx.enter_context(nc.psum_tensor("P", [128, 8, 512], F32))

        def banks(a, n, rows=128):
            return P[0:rows, a:a + n, :].rearrange("p b n -> p (b n)")

        xin_in, xres_in = sem("xin_in"), sem("xres_in")
        xT_done = sems("xT_done")
        dve_chain = sems("dve_chain")
        stat_done = sems("stat_done")
        var_done = sems("var_done")
        gs_done = sems("gs_done")
        pow_done = sems("pow_done")
        nb_done = sems("nb_done")
        xn_act, xn_dve = sems("xn_act"), sems("xn_dve")
        qk_done = sems("qk_done")
        hi_done, lo_done = sems("hi_done"), sems("lo_done")
        v_done = sems("v_done")
        vc_done = sems("vc_done")
        op_in = sems("op_in")
        rel_done, relhi_done, rello_done = sem("rel_done"), sem("relhi_done"), sem("rello_done")
        smax_done = sems("smax_done")
        smax_used = sems("smax_used")
        comb_done = sem("comb_done")
        mrow_in = [[sem(f"mrow_in{g}_l{n}") for g in range(G)] for n in range(2)]
        st_done = sems("st_done")
        p_done = sems("p_done")
        pv_done = sems("pv_done")
        o_done = sems("o_done")
        ot_done = sems("ot_done")
        rcp_done = sems("rcp_done")
        on_done = sems("on_done")
        ob_done = sems("ob_done")
        obc_done = sems("obc_done")
        y_done = sems("y_done")
        res_done = sems("res_done")
        x1_copied = sem("x1_copied")
        out_in = sem("out_in")
        PER_ITEMS = [G * (n + 1) for n in ITEMS]
        PER_STEPS = [G * n for n in STEPS]
        PER_UNITS = [G * n for n in UNITS]
        PER_OP = 24 * 16
        CHAIN = 5
        ROWS_IN = (6 + NH - 1 + 12) * 16
        w_in = sems("w_in")
        tab_in = sem("tab_in")
        scratch_zero = sem("scratch_zero")
        consts_done = sem("consts_done")
        rows_done = sem("rows_done")
        rows_in = sem("rows_in")
        tr_done = sem("tr_done")
        wt_done = sem("wt_done")
        kb_done = sem("kb_done")
        tab_done = sem("tab_done")
        tabhi_done = sem("tabhi_done")
        regT_done = sem("regT_done")
        reg_done = sem("reg_done")
        reghi_done = sem("reghi_done")
        regkv_done = sem("regkv_done")
        dve_set = sem("dve_set")
        pool_chain = sem("pool_chain")

        block = ctx.enter_context(nc.Block())

        SETUP_LOADS = 2 * (6 + 1 + 2 + 1)

        def qk_cols(t, k):
            return t[:, 0:2 * C].rearrange("p (g k c) -> p g k c", g=G, k=2)[:, :, k, :]

        def run_stages(eng, stage):
            for s in before_loop():
                stage(*s)
            with eng.Fori(1, B - 1) as i:
                for s in block_stages(i, i - 1, i + 1):
                    stage(*s)
            for s in after_loop():
                stage(*s)

        def consumed(job):
            kind, layer, image, group, n = job
            if kind == "rel":
                return rello_done, (image * G + group) * RELS + n + 1
            return smax_used[layer], image * PER_ITEMS[layer] + group * (ITEMS[layer] + 1) + n + 1

        def rel_views(at, g, n, *operands):
            heads = slice(GH * g, GH * g + GH)
            rows, cols = (P[r:r + 32, 4 + at % 2, :].rearrange("p (a h q) -> p a h q", a=4, h=GH) for r in (32, 64))
            yield (rows.rearrange("p a h q -> p h a q"),
                   *(t[32:64, heads, 128 * n:128 * n + 128].rearrange("p h (a q) -> p h a q", a=4) for t in operands))
            yield (cols.rearrange("p a h q -> p h q a"),
                   *(t[64:96, heads, 0:S].rearrange("p h (q w) -> p h q w", w=W)[:, :, :, 4 * n:4 * n + 4]
                     for t in operands))

        @block.sync
        def _(sp):
            sp.dma_start(xin[:], x_t[0]).then_inc(xin_in, 16)
            for n in range(2):
                if n:
                    sp.wait_ge(tr_done, 24)
                sp.dma_start(wnat, WQKV[n].rearrange("(m p) c -> p m c", p=GC)).then_inc(w_in[n], 16)
                sp.dma_start(wonat, WO[n].rearrange("(m p) c -> p m c", p=GC)).then_inc(w_in[n], 16)
                bias = BQKV[n].rearrange("(a n) -> a n", a=1)
                for k in range(2):
                    sp.dma_start(qk_cols(WT[n][CH:CH + 1, 1, :], k),
                                 bias[:, k * C:(k + 1) * C].rearrange("a (g c) -> a g c", g=G)).then_inc(w_in[n], 16)
                sp.dma_start(WT[n][CH:CH + 1, 1, 2 * C:3 * C], bias[:, 2 * C:3 * C]).then_inc(w_in[n], 16)
                sp.dma_start(WOT[n][CH:CH + 1, 1, :], BO[n].rearrange("(a n) -> a n", a=1)).then_inc(w_in[n], 16)
                if n == 0:
                    for k, t in enumerate((relh, relw)):
                        for half in range(2):
                            sp.dma_start(rtab[:, k, half * D:(half + 1) * D], t).then_inc(tab_in, 16)
                    sp.wait_ge(scratch_zero, 1)
                    for j in range(GH):
                        sp.dma_start(rnat[32 * j:32 * j + REG, :], regs).then_inc(tab_in, 16)
            sp.wait_ge(rows_done, 1)
            for r, n in ((32, 0), (64, 1)):
                sp.dma_start(K0[r:r + 32, :, :],
                             oneh[:, n:n + 1, :].broadcast_to((32, NH, S))).then_inc(rows_in, 16)
            for r, n in ((48, 0), (80, 1)):
                sp.dma_start(K1[r:r + 32, :, 0:S],
                             oneh[:, 2 + n:3 + n, :].broadcast_to((32, NH, S))).then_inc(rows_in, 16)
                sp.dma_start(A1[r:r + 32, :, :],
                             mask[:, n:n + 1, :].broadcast_to((32, NH, S))).then_inc(rows_in, 16)
            for h in range(NH):
                sp.dma_start(K1[112:113, h, :], ones).then_inc(rows_in if h < NH - 1 else out_in, 16)
            sp.wait_ge(regkv_done, 1)
            for r, src in ((0, rhi), (16, rlo), (32, rhi)):
                for j in range(GH):
                    sp.dma_start(K1[r:r + D, j:NH:GH, S:KW], src[D * j:D * j + D, :, :]).then_inc(rows_in, 16)

            def stage(kind, L, im, g, jobs):
                if kind == "prep":
                    sp.wait_ge(lo_done[L], im * G + G)
                    if L == 0:
                        copies = ((A0, 0, HI, 0), (A0, 16, HI, 0), (B0, 0, LO, 0), (B0, 16, LO, 0),
                                  (K0, 0, HI, 1), (K0, 16, LO, 1))
                    else:
                        copies = ((A1, 0, HI, 0), (A1, 16, HI, 0), (A1, 32, LO, 0),
                                  (K1, 0, HI, 1), (K1, 16, LO, 1), (K1, 32, HI, 1))
                    for dst, r, src, k in copies:
                        for j in range(GH):
                            row = k * GC + D * j
                            sp.dma_start(dst[r:r + D, j:NH:GH, 0:S], src[row:row + D, :, :]).then_inc(op_in[L], 16)
                for job in jobs[0][jobs[1]:jobs[2]]:
                    what, layer, image, group, n = job
                    if what == "max" and n == ITEMS[layer]:
                        sp.wait_ge(*consumed(job))
                        r = ROWS_MAX[layer]
                        sp.dma_start(A[layer][r:r + 1, GH * group:GH * group + GH, :],
                                     mrow[layer][:, group, :]).then_inc(mrow_in[layer][group], 16)
                if kind == "main" and L == 0 and g == 1:
                    sp.wait_ge(xT_done[1], im * 2)
                    sp.wait_ge(x1_copied, im)
                    sp.dma_start(xres[:], x_t[im]).then_inc(xres_in, 16)
                if kind == "main" and L == 0 and g == 2 and not (isinstance(im, int) and im == B - 1):
                    sp.wait_ge(xT_done[0], im * 2 + 2)
                    sp.dma_start(xin[:], x_t[im + 1]).then_inc(xin_in, 16)
                if kind == "out" and L == 1:
                    sp.wait_ge(res_done[1], im * 4 + 4)
                    sp.dma_start(out_t[im], x1[:]).then_inc(out_in, 16)

            run_stages(sp, stage)
            sp.wait_ge(out_in, 16 * B + 16)

        @block.gpsimd
        def _(pool):
            step = [0]

            def chained(ins):
                step[0] += 1
                ins.then_inc(pool_chain, 1)
                pool.wait_ge(pool_chain, step[0])

            nc.gpsimd.memset(rnat, 0.0).then_inc(scratch_zero, 1)
            nc.gpsimd.memset(negh[:], -0.5)
            nc.gpsimd.memset(epsc[:], EPS)
            chained(nc.gpsimd.memset(ident[:], 0.0))
            chained(nc.gpsimd.affine_select(out=ident[:], in_=ident[:], compare_op=ALU.not_equal, fill=1.0,
                                            base=0, pattern=[[-1, 128]], channel_multiplier=1))
            chained(nc.gpsimd.memset(flip, 0.0))
            chained(nc.gpsimd.affine_select(out=flip, in_=flip, compare_op=ALU.not_equal, fill=1.0,
                                            base=-62, pattern=[[1, 63]], channel_multiplier=1))
            chained(nc.gpsimd.memset(gmat[:], 1.0 / 6.0))
            gv = gmat[:].rearrange("p (a b) -> p a b", b=6)
            chained(nc.gpsimd.affine_select(out=gv, in_=gv, compare_op=ALU.is_ge, fill=0.0, base=0,
                                            pattern=[[-6, 16], [0, 6]], channel_multiplier=1))
            chained(nc.gpsimd.affine_select(out=gv, in_=gv, compare_op=ALU.is_ge, fill=0.0, base=5,
                                            pattern=[[6, 16], [0, 6]], channel_multiplier=-1))
            chained(nc.gpsimd.memset(notlo[:], -1.0))
            chained(nc.gpsimd.memset(notlo[0:D, :], 0.0))
            chained(nc.gpsimd.memset(regT[CH:CH + 1, :, :], 0.0))
            nc.gpsimd.memset(regT[CH:CH + 1, 1, :].rearrange("p (j r) -> p j r", j=GH)[:, :, 0:REG],
                             1.0).then_inc(consts_done, 1)
            for n, v in ((0, 1.0), (1, 1.0), (2, BIG), (3, BIG)):
                chained(nc.gpsimd.memset(oneh[:, n, :], v))
                o = oneh[:, n, :].rearrange("p (a b) -> p a b", b=W)
                pat = [[-1, H], [0, W]] if n % 2 == 0 else [[0, H], [-1, W]]
                chained(nc.gpsimd.affine_select(out=o, in_=o, compare_op=ALU.is_equal, fill=0.0, base=0,
                                                pattern=pat, channel_multiplier=1))
            R = WIN // 2
            for n in range(2):
                chained(nc.gpsimd.memset(mask[:, n, :], 0.0))
                m = mask[:, n, :].rearrange("p (a b) -> p a b", b=W)

                def select(lo, hi, base, step_q, cm):
                    sub = m[:, lo:hi, :] if n == 0 else m[:, :, lo:hi]
                    pat = [[step_q, hi - lo], [0, W]] if n == 0 else [[0, H], [step_q, hi - lo]]
                    chained(nc.gpsimd.affine_select(out=sub, in_=sub, compare_op=ALU.is_ge, fill=-BIG,
                                                    base=base, pattern=pat, channel_multiplier=cm))

                select(0, R + 1, WIN - 1, 0, -1)
                select(H - R - 1, H, WIN - H, 0, 1)
                select(R + 1, H - R - 1, R - (R + 1), -1, 1)
                select(R + 1, H - R - 1, R + (R + 1), 1, -1)
            nc.gpsimd.memset(ones, 1.0).then_inc(rows_done, 1)

            def take_wait():
                nc.gpsimd.tensor_tensor(negh[:, 1:2], negh[:, 0:1], negh[:, 2:3], ALU.mult)

            def stage(kind, L, im, g, jobs):
                if kind != "prep":
                    return
                pool.wait_ge(var_done[L], im + 1)
                nc.gpsimd.tensor_tensor(nrm[:, 1, :], nrm[:, 1, :], epsc[:], ALU.add).then_inc(pow_done[L], 1)
                pool.wait_ge(pow_done[L], im * 2 + 1)
                nc.gpsimd.tensor_tensor(nrm[:, 2, :], nrm[:, 1, :], negh[:, 2:4], ALU.pow).then_inc(pow_done[L], 1)
                if L == 1:
                    pool.wait_ge(res_done[0], im * 4 + 4)
                    pool.wait_ge(out_in, im * 16 + 16)
                    take_wait()
                    nc.gpsimd.tensor_copy(x1[:], xres[:]).then_inc(x1_copied, 1)

            run_stages(pool, stage)

        @block.scalar
        def _(act):
            def copy(out_, in_, scale=1.0):
                return nc.scalar.activation(out_, in_, ACT.Copy, scale=scale)

            for n in range(2):
                act.wait_ge(w_in[n], 16 * 6)
                kb = qk_cols(WT[n][CH:CH + 1, 1, :], 1)
                copy(kb, kb, D ** -0.5).then_inc(kb_done, 1)
                for t in range(24):
                    m, c = t // 2, t % 2
                    act.wait_ge(tr_done, 24 * n + t + 1)
                    if m < 6:
                        dst = qk_cols(WT[n][0:CH, c, :], m // G)[:, m % G, :]
                    elif m < 9:
                        dst = WT[n][0:CH, c, m * GC:(m + 1) * GC]
                    else:
                        dst = WOT[n][0:CH, c, (m - 9) * GC:(m - 8) * GC]
                    copy(dst, P[0:CH, t % 4, 0:GC], D ** -0.5 if m // G == 1 else 1.0).then_inc(wt_done, 1)
            prepared = []

            def stage(kind, L, im, g, jobs):
                if kind == "prep":
                    act.wait_ge(nb_done[L], im + 1)
                    nc.scalar.activation(xn[0:CH, 0, :], banks(0, 2, CH), ACT.Identity,
                                         bias=nrm[:, 3, 0:1], scale=nrm[:, 2, 0:1]).then_inc(xn_act[L], 1)
                    for m, b in enumerate((6, 4, 0)):
                        act.wait_ge(qk_done[L], im * G + m + 1)
                        copy(HI[:, m, :], banks(b, 2)).then_inc(hi_done[L], 1)
                    for n, b in enumerate((2, 3, 6, 7)):
                        act.wait_ge(v_done[L], im * 4 + n + 1)
                        copy(V[L][:, 2 * n:2 * n + 2, :, 0:D],
                             P[:, b, 0:2 * C].rearrange("p (t h d) -> p t h d", t=2, h=NH)).then_inc(vc_done[L], 1)
                    prepared.append((L, im))
                if kind == "jobs":
                    for at in range(*jobs[1:]):
                        high_part(jobs[0][at], at)
                if kind == "main":
                    base, ubase = im * PER_STEPS[L] + g * STEPS[L], im * PER_UNITS[L] + g * UNITS[L]
                    step = 0
                    after = paced(jobs, STEPS[L], SKIP[L])
                    for u in range(UNITS[L]):
                        if u >= RING or g:
                            act.wait_ge(pv_done[L], ubase + u - RING + 1)
                        for part in range(1 if L and u == 0 else 2):
                            for at in after[2 * step]:
                                high_part(jobs[0][at], at)
                            act.wait_ge(st_done[L], base + step + 1)
                            b = 2 * ((g * STEPS[L] + step) % 2)
                            n = 512 if L == 0 or u == 0 else W * (query_rows(u - 1)[1] - query_rows(u - 1)[0])
                            nc.scalar.activation(probs[:, (g * UNITS[L] + u) % RING, 2 * part:2 * part + 2, 0:n],
                                                 P[:, b:b + 2, 0:n], ACT.Exp).then_inc(p_done[L], 1)
                            for at in after[2 * step + 1]:
                                high_part(jobs[0][at], at)
                            step += 1
                        if L == 0 and u == TT + 1:
                            copy_out(L, im, g, ubase, 0)
                    for half in ((1,) if L == 0 else (0, 1)):
                        copy_out(L, im, g, ubase, half)
                if kind == "out":
                    for half in range(2):
                        act.wait_ge(ob_done[L], im * 2 + half + 1)
                        copy(xn[0:CH, :, half * 512:(half + 1) * 512],
                             P[0:CH, 2 * half:2 * half + 2, :]).then_inc(obc_done[L], 1)

            def high_part(job, at):
                if job[0] == "rel":
                    act.wait_ge(rel_done, consumed(job)[1])
                    for src, dst in rel_views(at, job[3], job[4], A0):
                        last = copy(dst, src)
                    last.then_inc(relhi_done, 1)

            def copy_out(L, im, g, ubase, half):
                while prepared:
                    pl, pi = prepared.pop()
                    act.wait_ge(op_in[pl], (pi + 1) * PER_OP)
                act.wait_ge(pv_done[L], ubase + ((half + 1) * TT if L == 0 else UNITS[1]))
                copy(oraw[:, g, half * 512:(half + 1) * 512], P[:, 6 + half, :]).then_inc(o_done[L], 1)

            run_stages(act, stage)

        @block.vector
        def _(dve):
            V_ = nc.vector
            V_.memset(xn[CH:CH + 1, :, :], 1.0)
            V_.memset(P[:, 6:8, :], 0.0)
            V_.memset(K0[96:97, :, :], 1.0)
            V_.memset(K1[0:64, :, S:KW], 0.0)
            V_.memset(K1[64:112, :, S:KW], 0.0)
            for n in range(2):
                V_.memset(V[n][:, :, :, D:D + 1], 1.0)
            V_.memset(vreg[:], 0.0).then_inc(dve_set, 1)
            dve.wait_ge(dve_set, 1)
            for j in range(GH):
                V_.memset(vreg[32 * j:32 * j + REG, :, 32 * j + D:32 * j + D + 1], 1.0).then_inc(dve_set, 1)
            dve.wait_ge(tab_done, 1)
            for k in range(2):
                V_.tensor_copy(ktmp[:, 64 * k:64 * k + 63], P[0:32, 4 + k, 0:63]).then_inc(tabhi_done, 1)
            dve.wait_ge(tabhi_done, 2)
            for k in range(2):
                V_.scalar_tensor_tensor(RT[:, k, 0:63], ktmp[:, 64 * k:64 * k + 63], notlo[:, 0:1],
                                        P[0:32, 4 + k, 0:63], ALU.mult, ALU.add)
            V_.tensor_copy(regT[0:CH, :, :], P[0:CH, 4:6, 128:256]).then_inc(regT_done, 1)
            dve.wait_ge(reg_done, 1)
            V_.tensor_copy(rhi, P[0:GC, 0:G, 0:32]).then_inc(reghi_done, 1)
            dve.wait_ge(reghi_done, 1)
            V_.tensor_tensor(rlo, P[0:GC, 0:G, 0:32], rhi, ALU.subtract)
            for j in range(GH):
                r = slice(32 * j, 32 * j + 32)
                last = V_.tensor_copy(vreg[r, :, 32 * j:32 * j + D],
                                      P[r, 3, 0:C].rearrange("p (g c) -> p g c", g=G)[:, :, D * j:D * j + D])
            last.then_inc(regkv_done, 1)

            def stage(kind, L, im, g, jobs):
                step = [0]

                def chained(ins):
                    step[0] += 1
                    ins.then_inc(dve_chain[L], 1)
                    dve.wait_ge(dve_chain[L], im * CHAIN + step[0])

                if kind == "prep":
                    for c in range(2):
                        dve.wait_ge(xT_done[L], im * 2 + c + 1)
                        for half in range(2):
                            ins = V_.bn_stats(bn[:, c, half, :], P[0:CH, 2 * c + half, :])
                    chained(ins)
                    V_.memset(nrm[:, 0, 0:1], 0.0)
                    for c in range(2):
                        ins = V_.bn_aggr(mv[:, c, :], bn[:, c, :, :].rearrange("p a b -> p (a b)"))
                    chained(ins)
                    chained(V_.tensor_tensor(nrm[:, 0, :], mv[:, :, 0], mv[:, :, 0], ALU.mult))
                    V_.tensor_tensor(st[:, :, 1], nrm[:, 0, :], mv[:, :, 1], ALU.add)
                    V_.tensor_copy(st[:, :, 0], mv[:, :, 0]).then_inc(stat_done[L], 1)
                    dve.wait_ge(gs_done[L], im + 1)
                    chained(V_.tensor_copy(gs[:].rearrange("p a b -> p (a b)"), P[0:CH, 4, 0:4]))
                    chained(V_.tensor_tensor(nrm[:, 0, :], gs[:, :, 0], gs[:, :, 0], ALU.mult))
                    V_.tensor_tensor(nrm[:, 1, :], gs[:, :, 1], nrm[:, 0, :], ALU.subtract).then_inc(var_done[L], 1)
                    dve.wait_ge(pow_done[L], im * 2 + 2)
                    V_.scalar_tensor_tensor(nrm[:, 3, :], gs[:, :, 0], -1.0, nrm[:, 2, :],
                                            ALU.mult, ALU.mult).then_inc(nb_done[L], 1)
                    dve.wait_ge(nb_done[L], im + 1)
                    V_.tensor_scalar(xn[0:CH, 1, :], banks(2, 2, CH), nrm[:, 2, 1:2], nrm[:, 3, 1:2],
                                     ALU.mult, ALU.add).then_inc(xn_dve[L], 1)
                    assert step[0] == 5
                    for m, b in enumerate((6, 4, 0)):
                        dve.wait_ge(hi_done[L], im * G + m + 1)
                        V_.tensor_tensor(LO[:, m, :], banks(b, 2), HI[:, m, :],
                                         ALU.subtract).then_inc(lo_done[L], 1)
                for at in range(*jobs[1:]):
                    job = jobs[0][at]
                    what, layer, image, group, n = job
                    used, value = consumed(job)
                    if what == "rel":
                        dve.wait_ge(relhi_done, value)
                        for src, low, high in rel_views(at, group, n, B0, A0):
                            last = V_.tensor_tensor(low, src, high, ALU.subtract)
                        last.then_inc(used, 1)
                        continue
                    dve.wait_ge(smax_done[layer], value)
                    bank = P[:, 4 + at % 2, :]
                    if n == ITEMS[layer]:
                        V_.tensor_scalar(mrow[layer][:, group, :], bank[0:GH * TT, 0:128], -1.0, None,
                                         ALU.mult).then_inc(used, 1)
                    elif layer == 0:
                        V_.reduce_max(mx[:, n // 2, n % 2:n % 2 + 1], bank, AX.X).then_inc(used, 1)
                        if n == ITEMS[0] - 1:
                            dve.wait_ge(used, value)
                            V_.tensor_reduce(mxc[:], mx[:], AX.X, ALU.max).then_inc(comb_done, 1)
                    else:
                        lo, hi = key_rows(n % TT)
                        V_.reduce_max(mxc[:, n:n + 1], bank[:, 0:W * (hi - lo) + REG], AX.X).then_inc(used, 1)
                if kind == "out":
                    for q in range(2):
                        dve.wait_ge(ot_done[L], im * TT + 4 * q + 4)
                        src = P[:, 4 * q:4 * q + 4, 0:NH * 32].rearrange("p t (h r) -> p t h r", r=32)
                        V_.reciprocal(rcp[:, q, :, :], src[:, :, :, D]).then_inc(rcp_done[L], 1)
                        dve.wait_ge(rcp_done[L], im * 2 + q + 1)
                        V_.tensor_tensor(onorm[:, 4 * q:4 * q + 4, :].rearrange("p t (h d) -> p t h d", h=NH),
                                         src[:, :, :, 0:D],
                                         rcp[:, q, :, :].unsqueeze(3).broadcast_to((128, 4, NH, D)),
                                         ALU.mult).then_inc(on_done[L], 1)
                    acc = xres if L == 0 else x1
                    if L == 0:
                        dve.wait_ge(xres_in, im * 16 + 16)
                    else:
                        dve.wait_ge(x1_copied, im + 1)
                    for b in range(4):
                        dve.wait_ge(y_done[L], im * 4 + b + 1)
                        V_.tensor_tensor(acc[:, 2 * b:2 * b + 2, :], P[:, 4 + b, 0:2 * C].rearrange("p (t c) -> p t c", t=2),
                                         acc[:, 2 * b:2 * b + 2, :], ALU.add).then_inc(res_done[L], 1)

            run_stages(dve, stage)

        @block.tensor
        def _(pe):
            mm = nc.tensor.matmul

            def chunks(out_, lhs, rhs):
                mm(out_, lhs(CH, 0), rhs(CH, 0), start=True, stop=False)
                return mm(out_, lhs(CH + 1, 1), rhs(CH + 1, 1), start=False, stop=True)

            pe.wait_ge(consts_done, 1)
            for n in range(2):
                pe.wait_ge(w_in[n], 16 * 6)
                for t in range(24):
                    m, c = t // 2, t % 2
                    if 24 * n + t >= 4:
                        pe.wait_ge(wt_done, 24 * n + t - 3)
                    src = wnat[:, m, :] if m < 9 else wonat[:, m - 9, :]
                    nc.tensor.transpose(P[0:CH, t % 4, 0:GC], src[:, c * CH:(c + 1) * CH],
                                        ident[0:GC, 0:GC]).then_inc(tr_done, 1)
                if n == 0:
                    pe.wait_ge(tab_in, 16 * 8)
                    for k in range(2):
                        mm(P[0:32, 4 + k, 0:63], rtab[:, k, :], flip, start=True, stop=True)
                        last = nc.tensor.transpose(P[0:CH, 4 + k, 128:256], rnat[:, k * CH:(k + 1) * CH], ident[:])
                    last.then_inc(tab_done, 1)
            pe.wait_ge(wt_done, 48)
            pe.wait_ge(kb_done, 2)
            pe.wait_ge(regT_done, 1)
            for g in range(G):
                chunks(P[0:GC, g, 0:32], lambda k, s: qk_cols(WT[1][0:k, s, :], 1)[:, g, :],
                       lambda k, s: regT[0:k, s, 0:32])
            chunks(P[:, 3, 0:C], lambda k, s: regT[0:k, s, :],
                   lambda k, s: WT[1][0:k, s, 2 * C:3 * C]).then_inc(reg_done, 1)
            pe.wait_ge(regkv_done, 1)
            pe.wait_ge(rows_in, ROWS_IN)
            pe.wait_ge(out_in, 16)

            def project(L, im):
                src = xin if L == 0 else xres
                if L == 0:
                    pe.wait_ge(xin_in, im * 16 + 16)
                else:
                    pe.wait_ge(res_done[0], im * 4 + 4)
                for c in range(2):
                    for t in range(TT):
                        last = nc.tensor.transpose(P[0:CH, 2 * c + t // 4, 128 * (t % 4):128 * (t % 4) + 128],
                                                   src[:, t, c * CH:(c + 1) * CH], ident[:])
                    last.then_inc(xT_done[L], 1)
                pe.wait_ge(stat_done[L], im + 1)
                mm(P[0:CH, 4, 0:4], gmat[:], st[:].rearrange("p a b -> p (a b)"),
                   start=True, stop=True).then_inc(gs_done[L], 1)
                pe.wait_ge(xn_act[L], im + 1)
                pe.wait_ge(xn_dve[L], im + 1)
                for m, b in enumerate((6, 4, 0)):
                    for half in range(2):
                        last = chunks(P[:, b + half, :], lambda k, s: WT[L][0:k, s, 128 * m:128 * m + 128],
                                      lambda k, s: xn[0:k, s, half * 512:(half + 1) * 512])
                    last.then_inc(qk_done[L], 1)
                for n, b in enumerate((2, 3, 6, 7)):
                    if n == 2:
                        pe.wait_ge(lo_done[L], im * G + 1)
                    for t in (2 * n, 2 * n + 1):
                        last = chunks(P[:, b, (t % 2) * C:(t % 2 + 1) * C],
                                      lambda k, s: xn[0:k, s, 128 * t:128 * t + 128],
                                      lambda k, s: WT[L][0:k, s, 2 * C:3 * C])
                    last.then_inc(v_done[L], 1)
                pe.wait_ge(lo_done[L], im * G + G)
                pe.wait_ge(vc_done[L], im * 4 + 4)

            def run_job(jobs, at):
                what, layer, image, group, n = jobs[0][at]
                if at >= 2:
                    pe.wait_ge(*consumed(jobs[0][at - 2]))
                if n == 0 and group == 0:
                    pe.wait_ge(op_in[layer], (image + 1) * PER_OP)
                if what == "rel":
                    mm(P[0:32, 4 + at % 2, 0:1], ident[:, 0:32], ident[:, 0:1], start=True, stop=True)
                    heads = slice(GH * group, GH * group + GH)
                    for a in range(4):
                        m = 4 * n + a
                        for q, first in ((A0, True), (B0, False)):
                            for k, rhs in enumerate((q[0:32, heads, W * m:W * m + W], q[0:32, heads, m:S:W])):
                                last = mm(P[32 + 32 * k:64 + 32 * k, 4 + at % 2, 128 * a:128 * a + 128],
                                          RT[:, k, H - 1 - m:2 * H - 1 - m], rhs, start=first, stop=not first)
                    last.then_inc(rel_done, 1)
                    return
                if layer == 0 and n == 0:
                    pe.wait_ge(rello_done, (image * G + group + 1) * RELS)
                bank = P[:, 4 + at % 2, :]
                if n == ITEMS[layer]:
                    if layer == 0:
                        pe.wait_ge(comb_done, image * G + group + 1)
                    else:
                        pe.wait_ge(*consumed(jobs[0][at - 1]))
                    last = nc.tensor.transpose(bank[0:GH * TT, 0:128], mxc[:], ident[:])
                elif layer == 0:
                    h, qt, half = GH * group + n // (2 * TT), n // 2 % TT, n % 2
                    last = mm(bank, A0[0:ROWS_MAX[0], h, 128 * qt:128 * qt + 128],
                              K0[0:ROWS_MAX[0], h, half * 512:(half + 1) * 512], start=True, stop=True)
                else:
                    h, qt = GH * group + n // TT, n % TT
                    lo, hi = key_rows(qt)
                    cols = W * (hi - lo)
                    lhs = A1[0:ROWS_MAX[1], h, 128 * qt:128 * qt + 128]
                    mm(bank[:, 0:cols], lhs, K1[0:ROWS_MAX[1], h, W * lo:W * hi], start=True, stop=True)
                    last = mm(bank[:, cols:cols + REG], lhs, K1[0:ROWS_MAX[1], h, S:S + REG], start=True, stop=True)
                last.then_inc(smax_done[layer], 1)

            def jobs_read(jobs):
                if jobs[2]:
                    pe.wait_ge(*consumed(jobs[0][jobs[2] - 1]))

            def attend(L, im, g, jobs):
                base, ubase = im * PER_STEPS[L] + g * STEPS[L], im * PER_UNITS[L] + g * UNITS[L]
                pe.wait_ge(mrow_in[L][g], im * 16 + 16)
                R = ROWS_MAX[L] + 1
                step = 0
                after = paced(jobs, STEPS[L], SKIP[L])
                ends = []

                def use(u):
                    pe.wait_ge(p_done[L], base + ends[u])
                    slot = (g * UNITS[L] + u) % RING
                    if g and u % (TT, UNITS[1])[L] == 0:
                        pe.wait_ge(o_done[L], im * 6 + 2 * g - (0 if L or u else 1))
                    if L == 0:
                        half, kt = u // TT, u % TT
                        for j in range(GH):
                            last = mm(P[32 * j:32 * j + D + 1, 6 + half, :], V[0][:, kt, GH * g + j, :],
                                      probs[:, slot, j, :], start=(kt == 0), stop=(kt == TT - 1))
                    elif u == 0:
                        for half in range(2):
                            last = mm(P[:, 6 + half, :], vreg[:, g, :], probs[:, slot, half, :],
                                      start=True, stop=False, skip_group_check=True)
                    else:
                        kt = u - 1
                        lo, hi = (W * r for r in query_rows(kt))
                        for half in range(2):
                            a, b = max(lo, 512 * half), min(hi, 512 * half + 512)
                            for j in range(GH if a < b else 0):
                                last = mm(P[32 * j:32 * j + D + 1, 6 + half, a - 512 * half:b - 512 * half],
                                          V[1][:, kt, GH * g + j, :], probs[:, slot, j, a - lo:b - lo],
                                          start=False, stop=(u == UNITS[1] - 1), skip_group_check=True)
                    last.then_inc(pv_done[L], 1)

                for u in range(UNITS[L]):
                    for part in range(1 if L and u == 0 else 2):
                        if step >= 2 or g:
                            pe.wait_ge(p_done[L], base + step - 1)
                        b = 2 * ((g * STEPS[L] + step) % 2)
                        if L == 1 and u == 0:
                            for half in range(2):
                                for j in range(GH):
                                    h = GH * g + j
                                    last = mm(P[32 * j:32 * j + 32, b + half, :], K1[0:R, h, S:KW],
                                              A1[0:R, h, 512 * half:512 * half + 512], start=True, stop=True)
                                for at in after[0] if half == 0 else ():
                                    run_job(jobs, at)
                        for jj in range(0 if L == 1 and u == 0 else 2):
                            for at in after[2 * step] if jj else ():
                                run_job(jobs, at)
                            h = GH * g + 2 * part + jj
                            if L == 0:
                                half, kt = u // TT, u % TT
                                q = slice(512 * half, 512 * half + 512)
                                k = slice(128 * kt, 128 * kt + 128)
                                mm(P[:, b + jj, :], K0[0:R, h, k], A0[0:R, h, q], start=True, stop=False)
                                last = mm(P[:, b + jj, :], K0[0:ROWS_LO, h, k], B0[0:ROWS_LO, h, q],
                                          start=False, stop=True)
                            else:
                                lo, hi = (W * r for r in query_rows(u - 1))
                                last = mm(P[:, b + jj, 0:hi - lo], K1[0:R, h, 128 * (u - 1):128 * u],
                                          A1[0:R, h, lo:hi], start=True, stop=True)
                        last.then_inc(st_done[L], 1)
                        for at in after[2 * step + 1]:
                            run_job(jobs, at)
                        step += 1
                    ends.append(step)
                    if u:
                        use(u - 1)
                use(UNITS[L] - 1)
                if g == G - 1:
                    jobs_read(jobs)
                    pe.wait_ge(o_done[L], im * 6 + 6)

            def deliver(L, im):
                for t in range(TT):
                    for g in range(G):
                        last = nc.tensor.transpose(P[:, t, 128 * g:128 * g + 128],
                                                   oraw[:, g, 128 * t:128 * t + 128], ident[:])
                    last.then_inc(ot_done[L], 1)
                for q in range(2):
                    pe.wait_ge(on_done[L], im * 2 + q + 1)
                    for t in range(4 * q, 4 * q + 4):
                        for c in range(2):
                            last = nc.tensor.transpose(P[0:CH, 2 * q + c, 128 * (t % 4):128 * (t % 4) + 128],
                                                       onorm[:, t, c * CH:(c + 1) * CH], ident[:])
                    last.then_inc(ob_done[L], 1)
                for b in range(4):
                    pe.wait_ge(obc_done[L], im * 2 + b // 2 + 1)
                    for t in (2 * b, 2 * b + 1):
                        last = chunks(P[:, 4 + b, (t % 2) * C:(t % 2 + 1) * C],
                                      lambda k, s: xn[0:k, s, 128 * t:128 * t + 128],
                                      lambda k, s: WOT[L][0:k, s, :])
                    last.then_inc(y_done[L], 1)
                pe.wait_ge(res_done[L], im * 4 + 4)

            def stage(kind, L, im, g, jobs):
                if kind == "prep":
                    project(L, im)
                if kind == "jobs":
                    for at in range(*jobs[1:]):
                        run_job(jobs, at)
                    jobs_read(jobs)
                if kind == "main":
                    attend(L, im, g, jobs)
                if kind == "out":
                    deliver(L, im)

            run_stages(pe, stage)


_INS = ["x", "L0_conv_w_qkv", "L0_conv_b_qkv", "L0_conv_w_proj", "L0_conv_b_proj", "L0_conv_rel_pos_h",
        "L0_conv_rel_pos_w", "L1_conv_registers", "L1_conv_qkv_w", "L1_conv_qkv_b", "L1_conv_out_w",
        "L1_conv_out_b"]


def kernel(**inputs):
    import numpy as _np
    import concourse.bacc as _bacc
    from concourse import mybir as _mybir
    from concourse.bass_utils import run_bass_kernel_spmd as _run

    nc = _bacc.Bacc("TRN2", target_bir_lowering=False, num_devices=1)
    arrays, args = {}, []
    for name in _INS:
        a = _np.ascontiguousarray(inputs[name])
        arrays[f"in_{name}_dram"] = a
        args.append(nc.dram_tensor(f"in_{name}_dram", a.shape, _mybir.dt.from_np(a.dtype), kind="ExternalInput").ap())
    out = nc.dram_tensor("out_0_dram", (B, H, W, C), _mybir.dt.float32, kind="ExternalOutput").ap()
    attention_kernel(nc, *args, out)
    r = _run(nc, [arrays], core_ids=[0])
    return r.results[0]["out_0_dram"]
```

```python
import concourse.bass as bass
from concourse import mybir
from contextlib import ExitStack

B, H, W, C = 16, 32, 32, 192
S = H * W
NH, D = 12, 16
G, GH = 3, 4
TT = S // 128
CH = C // 2
REG = 16
KW = S + 32
WIN = 7
EPS = 1e-5
BIG = 60000.0
ROWS_MAX = (96, 112)
ROWS_LO = 96
GC = GH * D
CG = C // 32
RELS = H // 4
UNITS = (16, 9)
STEPS = (64, 34)
ITEMS = (GH * TT * 2, GH * TT)
HALF_UNITS = ((TT, 2 * TT), (6, 9))
SKIP = (6, 0)
SCORES, JOBS = 3, 3
TAIL = 3
RING = 2


def is_image(image, n):
    return isinstance(image, int) and image == n


def start_row(q):
    return min(max(q - WIN // 2, 0), H - WIN)


def key_rows(qt):
    return start_row(4 * qt), start_row(4 * qt + 3) + WIN


def query_rows(kt):
    seen = [q for q in range(H) if start_row(q) <= 4 * kt + 3 and start_row(q) + WIN > 4 * kt]
    return seen[0], seen[-1] + 1


def max_jobs(layer, image, g):
    return [("max", layer, image, g, n) for n in range(ITEMS[layer] + 1)]


def rel_jobs(image, g):
    return [("rel", 0, image, g, n) for n in range(RELS)]


def stat_jobs(layer, image):
    return [("stat", layer, image, 0, n) for n in range(2)]


def among(jobs, few, at, step):
    out, before = [], 0
    for n, job in enumerate(few):
        here = int(len(jobs) * (at + n * step))
        out += jobs[before:here] + [job]
        before = here
    return out + jobs[before:]


def work(jobs):
    return sum({"rel": 12, "stat": 1, "max": (6, 4)[j[1]]}[j[0]] for j in jobs)


def spread(jobs, steps, first):
    after, at = [[] for _ in range(steps)], 0
    for k, job in enumerate(jobs):
        after[first + at * (steps - TAIL - first) // work(jobs)].append(k)
        at += work([job])
    return after


def mains(layer, image, *parts):
    steps, full = STEPS[layer], sum(parts, [])
    if len(parts) == 1:
        after = spread(full, G * steps, SKIP[layer])
    else:
        after, at = [], 0
        for g, part in enumerate(parts):
            after += [[at + k for k in ks] for ks in spread(part, steps, 0 if g else SKIP[layer])]
            at += len(part)
    for g in range(G):
        yield "main", layer, image, g, (full, after[steps * g:steps * (g + 1)])


def block_stages(i0, i1, n0):
    none = ([], [])
    coming = rel_jobs(n0, 0) + among(max_jobs(0, n0, 0), rel_jobs(n0, 1), 0.0, 1 / RELS) if n0 is not None else []
    if i0 is not None:
        coming = among(coming, stat_jobs(1, i0), 0.6, 0.1)
    first = [max_jobs(1, i1, g) for g in range(G)] if i1 is not None else [[]]
    if i1 is not None:
        yield "prep", 1, i1, None, none
    if i0 is not None:
        last = sum(first, [])
        if n0 is not None:
            yield "stats", 0, n0, None, none
            last = among(last, stat_jobs(0, n0), 0.4, 0.1)
        yield from mains(0, i0, among(max_jobs(0, i0, 1), rel_jobs(i0, 2), 0.0, 1 / RELS), max_jobs(0, i0, 2), last)
        yield "out", 0, i0, None, none
    else:
        yield "jobs", 1, i1, None, (first[0], [list(range(len(first[0])))])
    if n0 is not None:
        yield "prep", 0, n0, None, none
    if i0 is not None:
        yield "stats", 1, i0, None, none
    if i1 is not None:
        yield from mains(1, i1, coming) if i0 is not None else mains(1, i1, *first[1:], [])
        yield "out", 1, i1, None, none
    else:
        yield "jobs", 0, n0, None, (coming, [list(range(len(coming)))])


def before_loop():
    coming = rel_jobs(0, 0) + max_jobs(0, 0, 0) + rel_jobs(0, 1)
    yield "stats", 0, 0, None, ([], [])
    yield "jobs", 0, 0, None, (stat_jobs(0, 0), [[0, 1]])
    yield "prep", 0, 0, None, ([], [])
    yield "jobs", 0, 0, None, (coming, [list(range(len(coming)))])
    yield from block_stages(0, None, 1)


def after_loop():
    yield from block_stages(B - 1, B - 2, None)
    yield from block_stages(None, B - 1, None)


def attention_kernel(nc, x, wqkv0, bqkv0, wo0, bo0, relh, relw, regs, wqkv1, bqkv1, wo1, bo1, out):
    F32, F16 = mybir.dt.float32, mybir.dt.float16
    ALU, ACT, AX = mybir.AluOpType, mybir.ActivationFunctionType, mybir.AxisListType
    WQKV, BQKV, WO, BO = (wqkv0, wqkv1), (bqkv0, bqkv1), (wo0, wo1), (bo0, bo1)
    x_t = x.rearrange("b (t r) w c -> b (r w) t c", r=4)
    out_t = out.rearrange("b (t r) w c -> b (r w) t c", r=4)

    ctx = ExitStack()
    with ctx:
        def sb(name, shape, dt=F32):
            return ctx.enter_context(nc.sbuf_tensor(name, shape, dt))

        def sem(name):
            return ctx.enter_context(nc.semaphore(name))

        def sems(name):
            return [sem(f"{name}_l0"), sem(f"{name}_l1")]

        A0, B0, K0 = (sb(n, [128, NH, S], F16) for n in ("A0", "B0", "K0"))
        A1, K1 = sb("A1", [128, NH, S], F16), sb("K1", [128, NH, KW], F16)
        A = (A0, A1)
        V = [sb(f"V{n}", [128, TT, NH, D + 1]) for n in range(2)]
        vreg = sb("vreg", [128, G, 128])
        probs = sb("probs", [128, RING, GH, 512])
        onorm = probs[:, 0, 0:3, :].rearrange("p a n -> p (a n)").rearrange("p (t c) -> p t c", t=TT)
        xin = sb("xin", [128, TT, C])
        xres = sb("xres", [128, TT, C])
        x1 = sb("x1", [128, TT, C])
        xn = sb("xn", [CH + 1, 2, S])
        oraw = sb("oraw", [128, G, S])
        flat = oraw[:].rearrange("p g n -> p (g n)")
        HI = flat[:, 0:G * S // 2].bitcast(F16).rearrange("p (g n) -> p g n", g=G)
        LO = flat[:, G * S // 2:G * S].bitcast(F16).rearrange("p (g n) -> p g n", g=G)
        WT = [sb(f"WT{n}", [CH + 1, 2, 3 * C]) for n in range(2)]
        WOT = [sb(f"WOT{n}", [CH + 1, 2, C]) for n in range(2)]
        ident = sb("ident", [128, 128])
        gmat = sb("gmat", [CH, CH])
        RT = sb("RT", [32, 2, 64], F16)
        xsum = sb("xsum", [128, 2, C])
        xsq = sb("xsq", [128, C])
        onecol = sb("onecol", [128, 1])
        st = sb("st", [CH, 2, 2])
        gs = sb("gs", [CH, 2, 2])
        nrm = sb("nrm", [CH, 4, 2])
        epsc = sb("epsc", [CH, 2])
        negh = sb("negh", [CH, 2])
        scratch = sb("scratch", [CH, 5])
        negone = sb("negone", [CH, 2])
        mx = sb("mx", [128, GH * TT, 2])
        mxc = sb("mxc", [128, GH * TT])
        mrow = [sb(f"mrow{n}", [GH * TT, G, 128], F16) for n in range(2)]
        rcp = sb("rcp", [128, 2, 4, NH])
        notlo = sb("notlo", [32, 1])
        wnat = flat[0:GC, 0:9 * C].rearrange("p (m c) -> p m c", m=9)
        wonat = flat[0:GC, 9 * C:12 * C].rearrange("p (m c) -> p m c", m=3)
        rtab = flat[0:63, 12 * C:12 * C + 64].rearrange("p (k c) -> p k c", k=2)
        rnat = flat[:, 13 * C:14 * C]
        flip = flat[0:63, 14 * C:14 * C + 63]
        ktmp = xn[0:32, 0, 0:64].bitcast(F16)
        oneh = probs[0:32, 0, :, :].bitcast(F16).rearrange("p m n -> p (m n)").rearrange("p (m n) -> p m n", m=4)
        mask = probs[0:32, 1, :, :].bitcast(F16).rearrange("p m n -> p (m n)").rearrange("p (m n) -> p m n", m=4)
        ones = x1[0:1, :, :].bitcast(F16).rearrange("p t c -> p (t c)")[:, 0:KW]
        rhi = x1[0:GC, 4, 0:48].bitcast(F16).rearrange("p (g n) -> p g n", g=G)
        regT = x1[0:CH + 1, 6:8, 0:128]
        rlo = x1[0:GC, 5, 0:48].bitcast(F16).rearrange("p (g n) -> p g n", g=G)

        P = ctx.enter_context(nc.psum_tensor("P", [128, 8, 512], F32))

        def banks(a, n, rows=128):
            return P[0:rows, a:a + n, :].rearrange("p b n -> p (b n)")

        xin_in, xres_in = sem("xin_in"), sem("xres_in")
        pool_steps = sems("pool_steps")
        stat_done = sems("stat_done")
        stat_used = sems("stat_used")
        nb_done = sems("nb_done")
        xT_done = sems("xT_done")
        xn_act, xn_dve = sems("xn_act"), sems("xn_dve")
        qk_done = sems("qk_done")
        hi_done, lo_done = sems("hi_done"), sems("lo_done")
        v_done = sems("v_done")
        vc_done = sems("vc_done")
        q_in, k_in = ([[sem(f"{n}_l{m}_set{k}") for k in range(2)] for m in range(2)] for n in ("q_in", "k_in"))
        rel_done, relhi_done, rello_done = sem("rel_done"), sem("relhi_done"), sem("rello_done")
        smax_done = sems("smax_done")
        smax_used = sems("smax_used")
        comb_done = sem("comb_done")
        mrow_in = [[sem(f"mrow_in{g}_l{n}") for g in range(G)] for n in range(2)]
        st_done = sems("st_done")
        p_done = sems("p_done")
        pv_done = sems("pv_done")
        o_done = sems("o_done")
        ot_done = sems("ot_done")
        rcp_done = sems("rcp_done")
        on_done = sems("on_done")
        ob_done = sems("ob_done")
        obc_done = sems("obc_done")
        y_done = sems("y_done")
        res_done = sems("res_done")
        x1_copied = sem("x1_copied")
        out_in = sem("out_in")
        PER_ITEMS = [G * (n + 1) for n in ITEMS]
        PER_STEPS = [G * n for n in STEPS]
        PER_UNITS = [G * n for n in UNITS]
        PER_Q, PER_K = (16 * 16, 12 * 16), (8 * 16, 12 * 16)
        SUM_STEPS, POOL_STEPS = 3 * TT - 2, 3 * TT - 2 + 5
        ROWS_IN = (6 + NH - 1 + 12) * 16
        w_in = sems("w_in")
        tab_in = sem("tab_in")
        scratch_zero = sem("scratch_zero")
        consts_done = sem("consts_done")
        rows_done = sem("rows_done")
        rows_in = sem("rows_in")
        tr_done = sem("tr_done")
        wt_done = sem("wt_done")
        kb_done = sem("kb_done")
        tab_done = sem("tab_done")
        tabhi_done = sem("tabhi_done")
        regT_done = sem("regT_done")
        reg_done = sem("reg_done")
        reghi_done = sem("reghi_done")
        regkv_done = sem("regkv_done")
        dve_set = sem("dve_set")
        pool_chain = sem("pool_chain")

        block = ctx.enter_context(nc.Block())

        def qk_cols(t, k):
            return t[:, 0:2 * C].rearrange("p (g k c) -> p g k c", g=G, k=2)[:, :, k, :]

        def run_stages(eng, stage):
            for s in before_loop():
                stage(*s)
            with eng.Fori(1, B - 1) as i:
                for s in block_stages(i, i - 1, i + 1):
                    stage(*s)
            for s in after_loop():
                stage(*s)

        def consumed(job):
            kind, layer, image, group, n = job
            if kind == "rel":
                return rello_done, (image * G + group) * RELS + n + 1
            if kind == "stat":
                return stat_used[layer], image * 2 + n + 1
            return smax_used[layer], image * PER_ITEMS[layer] + group * (ITEMS[layer] + 1) + n + 1

        def job_bank(at):
            return SCORES + at % JOBS

        def rel_views(at, g, n, *operands):
            heads = slice(GH * g, GH * g + GH)
            rows, cols = (P[r:r + 32, job_bank(at), :].rearrange("p (a h q) -> p a h q", a=4, h=GH) for r in (32, 64))
            yield (rows.rearrange("p a h q -> p h a q"),
                   *(t[32:64, heads, 128 * n:128 * n + 128].rearrange("p h (a q) -> p h a q", a=4) for t in operands))
            yield (cols.rearrange("p a h q -> p h q a"),
                   *(t[64:96, heads, 0:S].rearrange("p h (q w) -> p h q w", w=W)[:, :, :, 4 * n:4 * n + 4]
                     for t in operands))

        def rows_to_operands(queue, L, im, part, copies, done, take_wait=None):
            def wait(ready, groups):
                queue.wait_ge(ready[L], im * G + groups)
                if take_wait:
                    take_wait((hi_done, lo_done).index(ready) + (0 if groups == 1 else 2))

            for k, (lo, hi) in enumerate(((0, 1), (1, G))):
                for n, (dst, r, src) in enumerate(copies):
                    if n == 0:
                        wait(hi_done, hi)
                    elif src is LO and copies[n - 1][2] is HI:
                        wait(lo_done, hi)
                    for j in range(GH):
                        row = part * GC + D * j
                        queue.dma_start(dst[r:r + D, GH * lo + j:GH * hi:GH, 0:S],
                                        src[row:row + D, lo:hi, :]).then_inc(done[k], 16)

        @block.sync
        def _(sp):
            sp.dma_start(xin[:], x_t[0]).then_inc(xin_in, 16)
            for n in range(2):
                if n:
                    sp.wait_ge(tr_done, 24)
                sp.dma_start(wnat, WQKV[n].rearrange("(m p) c -> p m c", p=GC)).then_inc(w_in[n], 16)
                sp.dma_start(wonat, WO[n].rearrange("(m p) c -> p m c", p=GC)).then_inc(w_in[n], 16)
                bias = BQKV[n].rearrange("(a n) -> a n", a=1)
                for k in range(2):
                    sp.dma_start(qk_cols(WT[n][CH:CH + 1, 1, :], k),
                                 bias[:, k * C:(k + 1) * C].rearrange("a (g c) -> a g c", g=G)).then_inc(w_in[n], 16)
                sp.dma_start(WT[n][CH:CH + 1, 1, 2 * C:3 * C], bias[:, 2 * C:3 * C]).then_inc(w_in[n], 16)
                sp.dma_start(WOT[n][CH:CH + 1, 1, :], BO[n].rearrange("(a n) -> a n", a=1)).then_inc(w_in[n], 16)
                if n == 0:
                    for k, t in enumerate((relh, relw)):
                        for half in range(2):
                            sp.dma_start(rtab[:, k, half * D:(half + 1) * D], t).then_inc(tab_in, 16)
                    sp.wait_ge(scratch_zero, 1)
                    for j in range(GH):
                        sp.dma_start(rnat[32 * j:32 * j + REG, :], regs).then_inc(tab_in, 16)

            def static_rows():
                sp.wait_ge(rows_done, 1)
                for r, n in ((32, 0), (64, 1)):
                    sp.dma_start(K0[r:r + 32, :, :],
                                 oneh[:, n:n + 1, :].broadcast_to((32, NH, S))).then_inc(rows_in, 16)
                for r, n in ((48, 0), (80, 1)):
                    sp.dma_start(K1[r:r + 32, :, 0:S],
                                 oneh[:, 2 + n:3 + n, :].broadcast_to((32, NH, S))).then_inc(rows_in, 16)
                    sp.dma_start(A1[r:r + 32, :, :],
                                 mask[:, n:n + 1, :].broadcast_to((32, NH, S))).then_inc(rows_in, 16)
                for h in range(NH):
                    sp.dma_start(K1[112:113, h, :], ones).then_inc(rows_in if h < NH - 1 else out_in, 16)
                sp.wait_ge(regkv_done, 1)
                for r, src in ((0, rhi), (16, rlo), (32, rhi)):
                    for j in range(GH):
                        sp.dma_start(K1[r:r + D, j:NH:GH, S:KW], src[D * j:D * j + D, :, :]).then_inc(rows_in, 16)

            def stage(kind, L, im, g, jobs):
                if kind == "prep":
                    rows_to_operands(sp, L, im, 0, (((A0, 0, HI), (A0, 16, HI), (B0, 0, LO), (B0, 16, LO)),
                                                    ((A1, 0, HI), (A1, 16, HI), (A1, 32, LO)))[L], q_in[L])
                    if L == 0 and is_image(im, 0):
                        static_rows()
                for at in sum(jobs[1], []):
                    job = jobs[0][at]
                    what, layer, image, group, n = job
                    if what == "max" and n == ITEMS[layer]:
                        sp.wait_ge(*consumed(job))
                        r = ROWS_MAX[layer]
                        sp.dma_start(A[layer][r:r + 1, GH * group:GH * group + GH, :],
                                     mrow[layer][:, group, :]).then_inc(mrow_in[layer][group], 16)
                if kind == "main" and L == 0 and g == 0 and not is_image(im, B - 1):
                    sp.wait_ge(xT_done[0], im * 4 + 4)
                    sp.dma_start(xin[:], x_t[im + 1]).then_inc(xin_in, 16)
                if kind == "main" and L == 0 and g == 1:
                    if not is_image(im, 0):
                        sp.wait_ge(xT_done[1], im * 4)
                        sp.wait_ge(x1_copied, im)
                    sp.dma_start(xres[:], x_t[im]).then_inc(xres_in, 16)
                if kind == "out" and L == 1:
                    sp.wait_ge(res_done[1], im * 4 + 4)
                    sp.dma_start(out_t[im], x1[:]).then_inc(out_in, 16)

            run_stages(sp, stage)
            sp.wait_ge(out_in, 16 * B + 16)

        @block.gpsimd
        def _(pool):
            step = [0]

            def chained(ins):
                step[0] += 1
                ins.then_inc(pool_chain, 1)
                pool.wait_ge(pool_chain, step[0])

            nc.gpsimd.memset(rnat, 0.0).then_inc(scratch_zero, 1)
            nc.gpsimd.memset(negh[:], -0.5)
            nc.gpsimd.memset(epsc[:], EPS)
            chained(nc.gpsimd.memset(ident[:], 0.0))
            chained(nc.gpsimd.affine_select(out=ident[:], in_=ident[:], compare_op=ALU.not_equal, fill=1.0,
                                            base=0, pattern=[[-1, 128]], channel_multiplier=1))
            chained(nc.gpsimd.memset(flip, 0.0))
            chained(nc.gpsimd.affine_select(out=flip, in_=flip, compare_op=ALU.not_equal, fill=1.0,
                                            base=-62, pattern=[[1, 63]], channel_multiplier=1))
            chained(nc.gpsimd.memset(gmat[:], 1.0 / (CG * S)))
            gv = gmat[:].rearrange("p (a b) -> p a b", b=CG)
            chained(nc.gpsimd.affine_select(out=gv, in_=gv, compare_op=ALU.is_ge, fill=0.0, base=0,
                                            pattern=[[-CG, CH // CG], [0, CG]], channel_multiplier=1))
            chained(nc.gpsimd.affine_select(out=gv, in_=gv, compare_op=ALU.is_ge, fill=0.0, base=CG - 1,
                                            pattern=[[CG, CH // CG], [0, CG]], channel_multiplier=-1))
            nc.gpsimd.memset(onecol[:], 1.0)
            nc.gpsimd.memset(negone[:], -1.0)
            chained(nc.gpsimd.memset(notlo[:], -1.0))
            chained(nc.gpsimd.memset(notlo[0:D, :], 0.0))
            chained(nc.gpsimd.memset(regT[CH:CH + 1, :, :], 0.0))
            nc.gpsimd.memset(regT[CH:CH + 1, 1, :].rearrange("p (j r) -> p j r", j=GH)[:, :, 0:REG],
                             1.0).then_inc(consts_done, 1)
            pool.wait_ge(consts_done, 1)

            def static_rows():
                for n, v in ((0, 1.0), (1, 1.0), (2, BIG), (3, BIG)):
                    chained(nc.gpsimd.memset(oneh[:, n, :], v))
                    o = oneh[:, n, :].rearrange("p (a b) -> p a b", b=W)
                    pat = [[-1, H], [0, W]] if n % 2 == 0 else [[0, H], [-1, W]]
                    chained(nc.gpsimd.affine_select(out=o, in_=o, compare_op=ALU.is_equal, fill=0.0, base=0,
                                                    pattern=pat, channel_multiplier=1))
                R = WIN // 2
                for n in range(2):
                    chained(nc.gpsimd.memset(mask[:, n, :], 0.0))
                    m = mask[:, n, :].rearrange("p (a b) -> p a b", b=W)

                    def select(lo, hi, base, step_q, cm):
                        sub = m[:, lo:hi, :] if n == 0 else m[:, :, lo:hi]
                        pat = [[step_q, hi - lo], [0, W]] if n == 0 else [[0, H], [step_q, hi - lo]]
                        chained(nc.gpsimd.affine_select(out=sub, in_=sub, compare_op=ALU.is_ge, fill=-BIG,
                                                        base=base, pattern=pat, channel_multiplier=cm))

                    select(0, R + 1, WIN - 1, 0, -1)
                    select(H - R - 1, H, WIN - H, 0, 1)
                    select(R + 1, H - R - 1, R - (R + 1), -1, 1)
                    select(R + 1, H - R - 1, R + (R + 1), 1, -1)
                nc.gpsimd.memset(ones, 1.0).then_inc(rows_done, 1)
                pool.wait_ge(rows_done, 1)

            def take_wait(n=4):
                nc.gpsimd.tensor_tensor(scratch[:, n:n + 1], negone[:, 0:1], negone[:, 1:2], ALU.mult)

            def statistics(L, im):
                tt, step = nc.gpsimd.tensor_tensor, [0]

                def counted(ins):
                    step[0] += 1
                    ins.then_inc(pool_steps[L], 1)

                def wait_steps():
                    pool.wait_ge(pool_steps[L], im * POOL_STEPS + step[0])

                if L == 0:
                    pool.wait_ge(xin_in, im * 16 + 16)
                else:
                    pool.wait_ge(res_done[0], im * 4 + 4)
                src = xres if L else xin
                counted(tt(xsum[:, 0, :], src[:, 0, :], src[:, 1, :], ALU.add))
                counted(tt(xsum[:, 1, :], src[:, 0, :], src[:, 0, :], ALU.mult))
                for t in range(1, TT):
                    if t > 1:
                        wait_steps()
                        counted(tt(xsum[:, 0, :], xsum[:, 0, :], src[:, t, :], ALU.add))
                    counted(tt(xsq[:], src[:, t, :], src[:, t, :], ALU.mult))
                    wait_steps()
                    counted(tt(xsum[:, 1, :], xsum[:, 1, :], xsq[:], ALU.add))
                assert step[0] == SUM_STEPS
                pool.wait_ge(stat_used[L], im * 2 + 2)
                counted(tt(nrm[:, 0, :], gs[:, :, 0], gs[:, :, 0], ALU.mult))
                wait_steps()
                counted(tt(nrm[:, 1, :], gs[:, :, 1], nrm[:, 0, :], ALU.subtract))
                wait_steps()
                counted(tt(nrm[:, 1, :], nrm[:, 1, :], epsc[:], ALU.add))
                wait_steps()
                counted(tt(nrm[:, 2, :], nrm[:, 1, :], negh[:], ALU.pow))
                wait_steps()
                counted(tt(nrm[:, 3, :], gs[:, :, 0], nrm[:, 2, :], ALU.mult))
                wait_steps()
                tt(nrm[:, 3, :], nrm[:, 3, :], negone[:], ALU.mult).then_inc(nb_done[L], 1)
                assert step[0] == POOL_STEPS

            def stage(kind, L, im, g, jobs):
                if kind == "stats":
                    statistics(L, im)
                    if L == 0 and is_image(im, 0):
                        static_rows()
                if kind == "prep":
                    rows_to_operands(pool, L, im, 1, (((K0, 0, HI), (K0, 16, LO)),
                                                      ((K1, 0, HI), (K1, 32, HI), (K1, 16, LO)))[L], k_in[L],
                                     take_wait)
                if kind == "prep" and L == 1:
                    pool.wait_ge(res_done[0], im * 4 + 4)
                    pool.wait_ge(out_in, im * 16 + 16)
                    take_wait()
                    nc.gpsimd.tensor_copy(x1[:], xres[:]).then_inc(x1_copied, 1)

            run_stages(pool, stage)

        @block.scalar
        def _(act):
            def copy(out_, in_, scale=1.0):
                return nc.scalar.activation(out_, in_, ACT.Copy, scale=scale)

            for n in range(2):
                act.wait_ge(w_in[n], 16 * 6)
                kb = qk_cols(WT[n][CH:CH + 1, 1, :], 1)
                copy(kb, kb, D ** -0.5).then_inc(kb_done, 1)
                for t in range(24):
                    m, c = t // 2, t % 2
                    act.wait_ge(tr_done, 24 * n + t + 1)
                    if m < 6:
                        dst = qk_cols(WT[n][0:CH, c, :], m // G)[:, m % G, :]
                    elif m < 9:
                        dst = WT[n][0:CH, c, m * GC:(m + 1) * GC]
                    else:
                        dst = WOT[n][0:CH, c, (m - 9) * GC:(m - 8) * GC]
                    copy(dst, P[0:CH, t % 4, 0:GC], D ** -0.5 if m // G == 1 else 1.0).then_inc(wt_done, 1)
            prepared = []

            def rows_moved():
                while prepared:
                    pl, pi = prepared.pop()
                    for k in range(2):
                        act.wait_ge(q_in[pl][k], (pi + 1) * PER_Q[pl])
                        act.wait_ge(k_in[pl][k], (pi + 1) * PER_K[pl])

            def stage(kind, L, im, g, jobs):
                if kind == "prep":
                    act.wait_ge(nb_done[L], im + 1)
                    for half in range(2):
                        act.wait_ge(xT_done[L], im * 4 + 2 * half + 1)
                        nc.scalar.activation(xn[0:CH, 0, 512 * half:512 * half + 512], P[0:CH, half, :], ACT.Identity,
                                             bias=nrm[:, 3, 0:1], scale=nrm[:, 2, 0:1]).then_inc(xn_act[L], 1)
                    for m, b in enumerate((6, 4, 0)):
                        act.wait_ge(qk_done[L], im * G + m + 1)
                        copy(HI[:, m, :], banks(b, 2)).then_inc(hi_done[L], 1)
                    for n, b in enumerate((2, 3, 6, 7)):
                        act.wait_ge(v_done[L], im * 4 + n + 1)
                        copy(V[L][:, 2 * n:2 * n + 2, :, 0:D],
                             P[:, b, 0:2 * C].rearrange("p (t h d) -> p t h d", t=2, h=NH)).then_inc(vc_done[L], 1)
                    prepared.append((L, im))
                if kind == "jobs":
                    for at in sum(jobs[1], []):
                        high_part(jobs[0][at], at)
                    rows_moved()
                if kind == "main":
                    base, ubase = im * PER_STEPS[L] + g * STEPS[L], im * PER_UNITS[L] + g * UNITS[L]
                    step = 0
                    after = jobs[1]
                    for u in range(UNITS[L]):
                        if u >= RING or g:
                            act.wait_ge(pv_done[L], ubase + u - RING + 1)
                        for j in range(2 if L and u == 0 else GH):
                            act.wait_ge(st_done[L], base + step + 1)
                            n = 512 if L == 0 or u == 0 else W * (query_rows(u - 1)[1] - query_rows(u - 1)[0])
                            nc.scalar.activation(probs[:, (g * UNITS[L] + u) % RING, j, 0:n],
                                                 P[:, (g * STEPS[L] + step) % SCORES, 0:n],
                                                 ACT.Exp).then_inc(p_done[L], 1)
                            for at in after[step]:
                                high_part(jobs[0][at], at)
                            step += 1
                        if u == HALF_UNITS[L][0] + 1:
                            copy_out(L, im, g, ubase, 0)
                    copy_out(L, im, g, ubase, 1)
                if kind == "out":
                    for half in range(2):
                        act.wait_ge(ob_done[L], im * 2 + half + 1)
                        copy(xn[0:CH, :, half * 512:(half + 1) * 512],
                             P[0:CH, 2 * half:2 * half + 2, :]).then_inc(obc_done[L], 1)

            def high_part(job, at):
                if job[0] == "rel":
                    act.wait_ge(rel_done, consumed(job)[1])
                    for src, dst in rel_views(at, job[3], job[4], A0):
                        copy(dst, src).then_inc(relhi_done, 1)

            def copy_out(L, im, g, ubase, half):
                rows_moved()
                act.wait_ge(pv_done[L], ubase + HALF_UNITS[L][half])
                copy(oraw[:, g, half * 512:(half + 1) * 512], P[:, 6 + half, :]).then_inc(o_done[L], 1)

            run_stages(act, stage)

        @block.vector
        def _(dve):
            V_ = nc.vector
            V_.memset(xn[CH:CH + 1, :, :], 1.0)
            V_.memset(P[:, 6:8, :], 0.0)
            V_.memset(K0[96:97, :, :], 1.0)
            V_.memset(K1[0:64, :, S:KW], 0.0)
            V_.memset(K1[64:112, :, S:KW], 0.0)
            for n in range(2):
                V_.memset(V[n][:, :, :, D:D + 1], 1.0)
            V_.memset(vreg[:], 0.0).then_inc(dve_set, 1)
            dve.wait_ge(dve_set, 1)
            for j in range(GH):
                V_.memset(vreg[32 * j:32 * j + REG, :, 32 * j + D:32 * j + D + 1], 1.0).then_inc(dve_set, 1)
            dve.wait_ge(tab_done, 1)
            for k in range(2):
                V_.tensor_copy(ktmp[:, 64 * k:64 * k + 63], P[0:32, 4 + k, 0:63]).then_inc(tabhi_done, 1)
            dve.wait_ge(tabhi_done, 2)
            for k in range(2):
                V_.scalar_tensor_tensor(RT[:, k, 0:63], ktmp[:, 64 * k:64 * k + 63], notlo[:, 0:1],
                                        P[0:32, 4 + k, 0:63], ALU.mult, ALU.add)
            V_.tensor_copy(regT[0:CH, :, :], P[0:CH, 4:6, 128:256]).then_inc(regT_done, 1)
            dve.wait_ge(reg_done, 1)
            V_.tensor_copy(rhi, P[0:GC, 0:G, 0:32]).then_inc(reghi_done, 1)
            dve.wait_ge(reghi_done, 1)
            V_.tensor_tensor(rlo, P[0:GC, 0:G, 0:32], rhi, ALU.subtract)
            for j in range(GH):
                r = slice(32 * j, 32 * j + 32)
                last = V_.tensor_copy(vreg[r, :, 32 * j:32 * j + D],
                                      P[r, 3, 0:C].rearrange("p (g c) -> p g c", g=G)[:, :, D * j:D * j + D])
            last.then_inc(regkv_done, 1)

            def stage(kind, L, im, g, jobs):
                if kind == "prep":
                    dve.wait_ge(nb_done[L], im + 1)
                    for half in range(2):
                        dve.wait_ge(xT_done[L], im * 4 + 2 * half + 2)
                        V_.tensor_scalar(xn[0:CH, 1, 512 * half:512 * half + 512], P[0:CH, 2 + half, :],
                                         nrm[:, 2, 1:2], nrm[:, 3, 1:2], ALU.mult, ALU.add).then_inc(xn_dve[L], 1)
                    for m, b in enumerate((6, 4, 0)):
                        dve.wait_ge(hi_done[L], im * G + m + 1)
                        V_.tensor_tensor(LO[:, m, :], banks(b, 2), HI[:, m, :],
                                         ALU.subtract).then_inc(lo_done[L], 1)
                for at in sum(jobs[1], []):
                    job = jobs[0][at]
                    what, layer, image, group, n = job
                    used, value = consumed(job)
                    if what == "rel":
                        for k, (src, low, high) in enumerate(rel_views(at, group, n, B0, A0)):
                            dve.wait_ge(relhi_done, 2 * value - 1 + k)
                            last = V_.tensor_tensor(low, src, high, ALU.subtract)
                        last.then_inc(used, 1)
                        continue
                    if what == "stat":
                        dve.wait_ge(stat_done[layer], value)
                        V_.tensor_copy((st, gs)[n][:].rearrange("p a b -> p (a b)"),
                                       P[0:CH, job_bank(at), 0:4]).then_inc(used, 1)
                        continue
                    dve.wait_ge(smax_done[layer], value)
                    bank = P[:, job_bank(at), :]
                    if n == ITEMS[layer]:
                        V_.tensor_scalar(mrow[layer][:, group, :], bank[0:GH * TT, 0:128], -1.0, None,
                                         ALU.mult).then_inc(used, 1)
                    elif layer == 0:
                        V_.reduce_max(mx[:, n // 2, n % 2:n % 2 + 1], bank, AX.X).then_inc(used, 1)
                        if n == ITEMS[0] - 1:
                            dve.wait_ge(used, value)
                            V_.tensor_reduce(mxc[:], mx[:], AX.X, ALU.max).then_inc(comb_done, 1)
                    else:
                        lo, hi = key_rows(n % TT)
                        V_.reduce_max(mxc[:, n:n + 1], bank[:, 0:W * (hi - lo) + REG], AX.X).then_inc(used, 1)
                if kind == "out":
                    dve.wait_ge(pv_done[L], im * PER_UNITS[L] + PER_UNITS[L])
                    for q in range(2):
                        dve.wait_ge(ot_done[L], im * TT + 4 * q + 4)
                        src = P[:, 4 * q:4 * q + 4, 0:NH * 32].rearrange("p t (h r) -> p t h r", r=32)
                        V_.reciprocal(rcp[:, q, :, :], src[:, :, :, D]).then_inc(rcp_done[L], 1)
                        dve.wait_ge(rcp_done[L], im * 2 + q + 1)
                        V_.tensor_tensor(onorm[:, 4 * q:4 * q + 4, :].rearrange("p t (h d) -> p t h d", h=NH),
                                         src[:, :, :, 0:D],
                                         rcp[:, q, :, :].unsqueeze(3).broadcast_to((128, 4, NH, D)),
                                         ALU.mult).then_inc(on_done[L], 1)
                    acc = xres if L == 0 else x1
                    if L == 0:
                        dve.wait_ge(xres_in, im * 16 + 16)
                    else:
                        dve.wait_ge(x1_copied, im + 1)
                    for b in range(4):
                        dve.wait_ge(y_done[L], im * 4 + b + 1)
                        y = P[:, 4 + b, 0:2 * C].rearrange("p (t c) -> p t c", t=2)
                        V_.tensor_tensor(acc[:, 2 * b:2 * b + 2, :], y, acc[:, 2 * b:2 * b + 2, :],
                                         ALU.add).then_inc(res_done[L], 1)

            run_stages(dve, stage)

        @block.tensor
        def _(pe):
            mm = nc.tensor.matmul

            def chunks(out_, lhs, rhs):
                mm(out_, lhs(CH, 0), rhs(CH, 0), start=True, stop=False)
                return mm(out_, lhs(CH + 1, 1), rhs(CH + 1, 1), start=False, stop=True)

            pe.wait_ge(consts_done, 1)
            for n in range(2):
                pe.wait_ge(w_in[n], 16 * 6)
                for t in range(24):
                    m, c = t // 2, t % 2
                    if 24 * n + t >= 4:
                        pe.wait_ge(wt_done, 24 * n + t - 3)
                    src = wnat[:, m, :] if m < 9 else wonat[:, m - 9, :]
                    nc.tensor.transpose(P[0:CH, t % 4, 0:GC], src[:, c * CH:(c + 1) * CH],
                                        ident[0:GC, 0:GC]).then_inc(tr_done, 1)
                if n == 0:
                    pe.wait_ge(tab_in, 16 * 8)
                    for k in range(2):
                        mm(P[0:32, 4 + k, 0:63], rtab[:, k, :], flip, start=True, stop=True)
                        last = nc.tensor.transpose(P[0:CH, 4 + k, 128:256], rnat[:, k * CH:(k + 1) * CH], ident[:])
                    last.then_inc(tab_done, 1)
            pe.wait_ge(wt_done, 48)
            pe.wait_ge(kb_done, 2)
            pe.wait_ge(regT_done, 1)
            for g in range(G):
                chunks(P[0:GC, g, 0:32], lambda k, s: qk_cols(WT[1][0:k, s, :], 1)[:, g, :],
                       lambda k, s: regT[0:k, s, 0:32])
            chunks(P[:, 3, 0:C], lambda k, s: regT[0:k, s, :],
                   lambda k, s: WT[1][0:k, s, 2 * C:3 * C]).then_inc(reg_done, 1)
            pe.wait_ge(regkv_done, 1)

            def project(L, im):
                src = xin if L == 0 else xres
                if L == 0:
                    pe.wait_ge(xin_in, im * 16 + 16)
                else:
                    pe.wait_ge(res_done[0], im * 4 + 4)
                for half in range(2):
                    for c in range(2):
                        for t in range(4):
                            last = nc.tensor.transpose(P[0:CH, 2 * c + half, 128 * t:128 * t + 128],
                                                       src[:, 4 * half + t, c * CH:(c + 1) * CH], ident[:])
                        last.then_inc(xT_done[L], 1)
                y_read()
                for m, b in enumerate((6, 4, 0)):
                    for half in range(2):
                        if m == 0:
                            pe.wait_ge(xn_act[L], im * 2 + half + 1)
                            pe.wait_ge(xn_dve[L], im * 2 + half + 1)
                        last = chunks(P[:, b + half, :], lambda k, s: WT[L][0:k, s, 128 * m:128 * m + 128],
                                      lambda k, s: xn[0:k, s, half * 512:(half + 1) * 512])
                    last.then_inc(qk_done[L], 1)
                for n, b in enumerate((2, 3, 6, 7)):
                    if n == 2:
                        pe.wait_ge(lo_done[L], im * G + 1)
                    for t in (2 * n, 2 * n + 1):
                        last = chunks(P[:, b, (t % 2) * C:(t % 2 + 1) * C],
                                      lambda k, s: xn[0:k, s, 128 * t:128 * t + 128],
                                      lambda k, s: WT[L][0:k, s, 2 * C:3 * C])
                    last.then_inc(v_done[L], 1)
                unread_qkv.append((L, im))

            unread_y, unread_qkv = [], []

            def y_read():
                while unread_y:
                    yl, yi = unread_y.pop()
                    pe.wait_ge(res_done[yl], yi * 4 + 4)

            def banks_read(k):
                for ql, qi in unread_qkv:
                    if k == 0:
                        pe.wait_ge(lo_done[ql], qi * G + G)
                    else:
                        pe.wait_ge(vc_done[ql], qi * 4 + 2 * k)
                if k == 2:
                    unread_qkv.clear()

            def run_job(jobs, at):
                what, layer, image, group, n = jobs[0][at]
                if at >= JOBS:
                    pe.wait_ge(*consumed(jobs[0][at - JOBS]))
                if what == "stat":
                    bank = P[0:CH, job_bank(at), :]
                    if n == 0:
                        pe.wait_ge(pool_steps[layer], image * POOL_STEPS + SUM_STEPS)
                        for c in range(2):
                            for k in range(2):
                                last = mm(bank[:, 2 * c + k:2 * c + k + 1], xsum[:, k, c * CH:(c + 1) * CH],
                                          onecol[:], start=True, stop=True)
                    else:
                        pe.wait_ge(*consumed(jobs[0][at][:4] + (0,)))
                        last = mm(bank[:, 0:4], gmat[:], st[:].rearrange("p a b -> p (a b)"), start=True, stop=True)
                    last.then_inc(stat_done[layer], 1)
                    return
                if n == 0 and group < 2:
                    pe.wait_ge(q_in[layer][group], (image + 1) * PER_Q[layer])
                    if what == "max":
                        pe.wait_ge(k_in[layer][group], (image + 1) * PER_K[layer])
                    if what == "max" and layer == 0 and is_image(image, 0):
                        pe.wait_ge(rows_in, ROWS_IN)
                        pe.wait_ge(out_in, 16)
                if what == "rel":
                    mm(P[0:32, job_bank(at), 0:1], ident[:, 0:32], ident[:, 0:1], start=True, stop=True)
                    heads = slice(GH * group, GH * group + GH)
                    for a in range(4):
                        m = 4 * n + a
                        for q, first in ((A0, True), (B0, False)):
                            for k, rhs in enumerate((q[0:32, heads, W * m:W * m + W], q[0:32, heads, m:S:W])):
                                last = mm(P[32 + 32 * k:64 + 32 * k, job_bank(at), 128 * a:128 * a + 128],
                                          RT[:, k, H - 1 - m:2 * H - 1 - m], rhs, start=first, stop=not first)
                    last.then_inc(rel_done, 1)
                    return
                if layer == 0 and n == 0:
                    pe.wait_ge(rello_done, (image * G + group + 1) * RELS)
                bank = P[:, job_bank(at), :]
                if n == ITEMS[layer]:
                    if layer == 0:
                        pe.wait_ge(comb_done, image * G + group + 1)
                    else:
                        pe.wait_ge(*consumed(jobs[0][at - 1]))
                    last = nc.tensor.transpose(bank[0:GH * TT, 0:128], mxc[:], ident[:])
                elif layer == 0:
                    h, qt, half = GH * group + n // (2 * TT), n // 2 % TT, n % 2
                    last = mm(bank, A0[0:ROWS_MAX[0], h, 128 * qt:128 * qt + 128],
                              K0[0:ROWS_MAX[0], h, half * 512:(half + 1) * 512], start=True, stop=True)
                else:
                    h, qt = GH * group + n // TT, n % TT
                    lo, hi = key_rows(qt)
                    cols = W * (hi - lo)
                    lhs = A1[0:ROWS_MAX[1], h, 128 * qt:128 * qt + 128]
                    mm(bank[:, 0:cols], lhs, K1[0:ROWS_MAX[1], h, W * lo:W * hi], start=True, stop=True)
                    last = mm(bank[:, cols:cols + REG], lhs, K1[0:ROWS_MAX[1], h, S:S + REG], start=True, stop=True)
                last.then_inc(smax_done[layer], 1)

            def jobs_read(jobs):
                if jobs[0]:
                    pe.wait_ge(*consumed(jobs[0][-1]))

            def attend(L, im, g, jobs):
                base, ubase = im * PER_STEPS[L] + g * STEPS[L], im * PER_UNITS[L] + g * UNITS[L]
                pe.wait_ge(mrow_in[L][g], im * 16 + 16)
                y_read()
                R = ROWS_MAX[L] + 1
                step = 0
                after = jobs[1]
                ends = []

                def use(u):
                    pe.wait_ge(p_done[L], base + ends[u])
                    slot = (g * UNITS[L] + u) % RING
                    if g == 0 and u == 0:
                        banks_read(2)
                    if g and u % (TT, UNITS[1])[L] == 0:
                        pe.wait_ge(o_done[L], im * 6 + 2 * g - (0 if L or u else 1))
                    if L == 0:
                        half, kt = u // TT, u % TT
                        for j in range(GH):
                            last = mm(P[32 * j:32 * j + D + 1, 6 + half, :], V[0][:, kt, GH * g + j, :],
                                      probs[:, slot, j, :], start=(kt == 0), stop=(kt == TT - 1))
                    elif u == 0:
                        for half in range(2):
                            last = mm(P[:, 6 + half, :], vreg[:, g, :], probs[:, slot, half, :],
                                      start=True, stop=False, skip_group_check=True)
                    else:
                        kt = u - 1
                        lo, hi = (W * r for r in query_rows(kt))
                        for half in range(2):
                            a, b = max(lo, 512 * half), min(hi, 512 * half + 512)
                            for j in range(GH if a < b else 0):
                                last = mm(P[32 * j:32 * j + D + 1, 6 + half, a - 512 * half:b - 512 * half],
                                          V[1][:, kt, GH * g + j, :], probs[:, slot, j, a - lo:b - lo],
                                          start=False, stop=(u == HALF_UNITS[1][half] - 1), skip_group_check=True)
                    last.then_inc(pv_done[L], 1)

                for u in range(UNITS[L]):
                    for j in range(2 if L and u == 0 else GH):
                        if step >= SCORES or g:
                            pe.wait_ge(p_done[L], base + step - SCORES + 1)
                        if g == 0 and step == 0:
                            banks_read(0)
                        bank, h = P[:, (g * STEPS[L] + step) % SCORES, :], GH * g + j
                        if L == 0:
                            half, kt = u // TT, u % TT
                            q = slice(512 * half, 512 * half + 512)
                            k = slice(128 * kt, 128 * kt + 128)
                            mm(bank, K0[0:R, h, k], A0[0:R, h, q], start=True, stop=False)
                            last = mm(bank, K0[0:ROWS_LO, h, k], B0[0:ROWS_LO, h, q], start=False, stop=True)
                        elif u == 0:
                            for jj in range(GH):
                                last = mm(bank[32 * jj:32 * jj + 32, :], K1[0:R, GH * g + jj, S:KW],
                                          A1[0:R, GH * g + jj, 512 * j:512 * j + 512], start=True, stop=True)
                        else:
                            lo, hi = (W * r for r in query_rows(u - 1))
                            last = mm(bank[:, 0:hi - lo], K1[0:R, h, 128 * (u - 1):128 * u],
                                      A1[0:R, h, lo:hi], start=True, stop=True)
                        last.then_inc(st_done[L], 1)
                        if g == 0 and step == 0:
                            banks_read(1)
                        for at in after[step]:
                            run_job(jobs, at)
                        step += 1
                    ends.append(step)
                    if u:
                        use(u - 1)
                use(UNITS[L] - 1)
                if g == G - 1:
                    jobs_read(jobs)

            def deliver(L, im):
                for t in range(TT):
                    if t % 4 == 0:
                        pe.wait_ge(o_done[L], im * 6 + 5 + t // 4)
                    for g in range(G):
                        last = nc.tensor.transpose(P[:, t, 128 * g:128 * g + 128],
                                                   oraw[:, g, 128 * t:128 * t + 128], ident[:])
                    last.then_inc(ot_done[L], 1)
                for q in range(2):
                    pe.wait_ge(on_done[L], im * 2 + q + 1)
                    for t in range(4 * q, 4 * q + 4):
                        for c in range(2):
                            last = nc.tensor.transpose(P[0:CH, 2 * q + c, 128 * (t % 4):128 * (t % 4) + 128],
                                                       onorm[:, t, c * CH:(c + 1) * CH], ident[:])
                    last.then_inc(ob_done[L], 1)
                for b in range(4):
                    pe.wait_ge(obc_done[L], im * 2 + b // 2 + 1)
                    for t in (2 * b, 2 * b + 1):
                        last = chunks(P[:, 4 + b, (t % 2) * C:(t % 2 + 1) * C],
                                      lambda k, s: xn[0:k, s, 128 * t:128 * t + 128],
                                      lambda k, s: WOT[L][0:k, s, :])
                    last.then_inc(y_done[L], 1)
                if L == 0:
                    unread_y.append((L, im))
                else:
                    pe.wait_ge(res_done[L], im * 4 + 4)

            def stage(kind, L, im, g, jobs):
                if kind == "prep":
                    project(L, im)
                if kind == "jobs":
                    for k in range(3 if unread_qkv else 0):
                        banks_read(k)
                    for at in sum(jobs[1], []):
                        run_job(jobs, at)
                    jobs_read(jobs)
                if kind == "main":
                    attend(L, im, g, jobs)
                if kind == "out":
                    deliver(L, im)

            run_stages(pe, stage)


_INS = ["x", "L0_conv_w_qkv", "L0_conv_b_qkv", "L0_conv_w_proj", "L0_conv_b_proj", "L0_conv_rel_pos_h",
        "L0_conv_rel_pos_w", "L1_conv_registers", "L1_conv_qkv_w", "L1_conv_qkv_b", "L1_conv_out_w",
        "L1_conv_out_b"]


def kernel(**inputs):
    import numpy as _np
    import concourse.bacc as _bacc
    from concourse import mybir as _mybir
    from concourse.bass_utils import run_bass_kernel_spmd as _run

    nc = _bacc.Bacc("TRN2", target_bir_lowering=False, num_devices=1)
    arrays, args = {}, []
    for name in _INS:
        a = _np.ascontiguousarray(inputs[name])
        arrays[f"in_{name}_dram"] = a
        args.append(nc.dram_tensor(f"in_{name}_dram", a.shape, _mybir.dt.from_np(a.dtype), kind="ExternalInput").ap())
    out = nc.dram_tensor("out_0_dram", (B, H, W, C), _mybir.dt.float32, kind="ExternalOutput").ap()
    attention_kernel(nc, *args, out)
    r = _run(nc, [arrays], core_ids=[0])
    return r.results[0]["out_0_dram"]
```
